# Optimizing a Trainium2 kernel written in Bass

```python
import numpy as np
import jax
import jax.numpy as jnp

def _softmax(x, axis=-1):
    return jax.nn.softmax(x, axis=axis)

def _gelu(x):
    return jax.nn.gelu(x, approximate=True)

def _silu(x):
    return jax.nn.silu(x)

def _sigmoid(x):
    return jax.nn.sigmoid(x)

def _layernorm(x, axis=-1, eps=1e-05):
    m = jnp.mean(x, axis=axis, keepdims=True)
    v = jnp.var(x, axis=axis, keepdims=True)
    return (x - m) / jnp.sqrt(v + eps)

def _scatter_add(tgt, idx, src, axis=0):
    return tgt.at[idx].add(src)

def _segment_sum(src, seg, n):
    return jax.ops.segment_sum(src, seg, n)
kernel_name = 'mk_macaron_d1_jaxref_r4_401141'

def setup_inputs(seed: int=0):
    np.random.seed(seed)
    _w = jnp.asarray

    def _L0_attn_setup():
        import jax, jax.numpy as jnp
        import numpy as np
        B, L, D, H = (2, 512, 256, 16)
        d = D // H
        key = jax.random.key(seed)
        ks = jax.random.split(key, 6)
        X = jax.random.normal(ks[0], (B, L, D), dtype=jnp.float32)
        scale = 0.02
        Wq = scale * jax.random.normal(ks[1], (D, D), dtype=jnp.float32)
        Wk = scale * jax.random.normal(ks[2], (D, D), dtype=jnp.float32)
        Wv = scale * jax.random.normal(ks[3], (D, D), dtype=jnp.float32)
        Wc = scale * jax.random.normal(ks[4], (D, D), dtype=jnp.float32)
        Ltri = scale * jax.random.normal(ks[5], (H, d, d), dtype=jnp.float32)
        return {'X': X, 'Wq': Wq, 'Wk': Wk, 'Wv': Wv, 'Wc': Wc, 'Ltri': Ltri}
    _L0_attn_in = _L0_attn_setup()

    def _L0_ffn_setup():
        import math
        import jax, jax.numpy as jnp
        import numpy as np
        TOP_K = 2
        CAP_FACTOR = 1.25
        CLAMP = 10000.0
        key = jax.random.key(seed)
        k1, k2, k3, k4, k5 = jax.random.split(key, 5)
        B, S, D, F, E = (4, 512, 256, 1024, 8)
        std = 0.02
        return {'x': jax.random.normal(k1, (B, S, D), dtype=jnp.float32), 'Wr': jax.random.normal(k2, (D, E), dtype=jnp.float32) * std, 'W1': jax.random.normal(k3, (E, D, F), dtype=jnp.float32) * std, 'W3': jax.random.normal(k4, (E, D, F), dtype=jnp.float32) * std, 'W2': jax.random.normal(k5, (E, F, D), dtype=jnp.float32) * std}
    _L0_ffn_in = _L0_ffn_setup()
    _d = {'L0_attn_X': _L0_attn_in['X'], 'L0_attn_Wq': _L0_attn_in['Wq'], 'L0_attn_Wk': _L0_attn_in['Wk'], 'L0_attn_Wv': _L0_attn_in['Wv'], 'L0_attn_Wc': _L0_attn_in['Wc'], 'L0_attn_Ltri': _L0_attn_in['Ltri'], 'L0_ffn_Wr': _L0_ffn_in['Wr'], 'L0_ffn_W1': _L0_ffn_in['W1'], 'L0_ffn_W3': _L0_ffn_in['W3'], 'L0_ffn_W2': _L0_ffn_in['W2']}
    _x0 = _d['L0_attn_X']
    _d['L0_attn_X'] = jax.random.normal(jax.random.fold_in(jax.random.key(seed), 1), (4, 2048, 256), dtype=_x0.dtype)
    del _x0
    return _d

def reference(L0_attn_X, L0_attn_Wq, L0_attn_Wk, L0_attn_Wv, L0_attn_Wc, L0_attn_Ltri, L0_ffn_Wr, L0_ffn_W1, L0_ffn_W3, L0_ffn_W2):

    def _L0_attn_ref(X, Wq, Wk, Wv, Wc, Ltri):
        import jax, jax.numpy as jnp
        import numpy as np
        B, L, D, H = (2, 512, 256, 16)
        d = D // H
        Bsz, Lq, Dm = X.shape
        Q = (X @ Wq.T).reshape(Bsz, Lq, H, d)
        K = (X @ Wk.T).reshape(Bsz, Lq, H, d)
        V = (X @ Wv.T).reshape(Bsz, Lq, H, d)
        KV = jnp.einsum('blhd,blhe->blhde', K, V)
        KVc = jnp.cumsum(KV, axis=1)
        Y = jnp.einsum('blhd,blhde->blhe', Q, KVc)
        mask = jnp.tril(jnp.ones((1, d, d), dtype=X.dtype))
        Lm = Ltri * mask
        Bm = Lm @ jnp.swapaxes(Lm, -2, -1)
        Y = jnp.einsum('hed,blhd->blhe', Bm, Y)
        Y = Y.reshape(Bsz, Lq, Dm)
        return Y @ Wc.T

    def _L0_ffn_ref(x, Wr, W1, W3, W2):
        import math
        import jax, jax.numpy as jnp
        import numpy as np
        TOP_K = 2
        CAP_FACTOR = 1.25
        CLAMP = 10000.0
        B, S, D = x.shape
        E = Wr.shape[1]
        K = TOP_K
        T = B * S
        cap = max(1, math.ceil(T * K * CAP_FACTOR / E))
        xf = x.reshape(T, D)
        logits = jnp.clip(xf @ Wr, -CLAMP, CLAMP)
        top_v, top_i = jax.lax.top_k(logits, K)
        m = jnp.max(top_v, axis=-1, keepdims=True)
        expv = jnp.exp(top_v - m)
        top_p = expv / (jnp.sum(expv, axis=-1, keepdims=True) + 1e-12)
        Sp = T * K
        experts = top_i.reshape(Sp)
        weights = top_p.reshape(Sp)
        tokens = jnp.repeat(jnp.arange(T), K)
        oh = experts[:, None] == jnp.arange(E)[None, :]
        pos = jnp.sum(jnp.cumsum(oh.astype(jnp.int32), axis=0) * oh, axis=-1) - 1
        kept = pos < cap
        pos_safe = jnp.where(kept, pos, cap)
        xe = jnp.zeros((E, cap + 1, D), x.dtype).at[experts, pos_safe].set(xf[tokens])[:, :cap]
        h = jax.nn.silu(jnp.einsum('ecd,edf->ecf', xe, W1)) * jnp.einsum('ecd,edf->ecf', xe, W3)
        ye = jnp.einsum('ecf,efd->ecd', h, W2)
        yp = ye[experts, jnp.minimum(pos_safe, cap - 1)]
        wk = weights * kept.astype(weights.dtype)
        out = jnp.zeros((T, D), x.dtype).at[tokens].add(wk[:, None] * yp)
        return out.reshape(B, S, D)
    x = L0_attn_X
    x = x + 0.5 * _L0_ffn_ref(_layernorm(x, axis=-1), L0_ffn_Wr, L0_ffn_W1, L0_ffn_W3, L0_ffn_W2)
    x = x + _L0_attn_ref(_layernorm(x, axis=-1), L0_attn_Wq, L0_attn_Wk, L0_attn_Wv, L0_attn_Wc, L0_attn_Ltri)
    x = x + 0.5 * _L0_ffn_ref(_layernorm(x, axis=-1), L0_ffn_Wr, L0_ffn_W1, L0_ffn_W3, L0_ffn_W2)
    return x

_drawn_inputs = setup_inputs


def setup_inputs(seed=0):
    import zlib

    import numpy as np

    out = dict(_drawn_inputs(seed))
    spreads = {}
    factors = {'L0_attn_Wq': 3.036,
     'L0_attn_Wk': 2.973,
     'L0_attn_Wv': 3.026,
     'L0_attn_Wc': 2.998,
     'L0_attn_Ltri': 4.086,
     'L0_ffn_Wr': 12.063,
     'L0_ffn_W1': 3.937,
     'L0_ffn_W3': 3.898,
     'L0_ffn_W2': 3.884}
    for name, (base, spread) in spreads.items():
        noise = np.random.default_rng([zlib.crc32(name.encode()), seed]).standard_normal(out[name].shape)
        drawn = base * np.exp(spread * noise) if base else spread * noise
        out[name] = jnp.asarray(drawn.astype(out[name].dtype))
    for name, factor in factors.items():
        out[name] = (out[name] * factor).astype(out[name].dtype)
    return out
```

```python
from contextlib import ExitStack

import concourse.bass as bass
from concourse import mybir

F32 = mybir.dt.float32
F32R = mybir.dt.float32r
BF16 = mybir.dt.bfloat16
I32 = mybir.dt.int32
U32 = mybir.dt.uint32
ALU = mybir.AluOpType
ACT = mybir.ActivationFunctionType
AX_X = mybir.AxisListType.X

P = 128
T = 4 * 2048
D = 256
KD = D // P
E = 8
TOPK = 2
F = 1024
KF = F // P
CAP = -(-T * TOPK * 5 // (4 * E))
H = 16
HD = D // H
HH = P // HD
NC = 4
GT = NC * P
G = T // GT
GB = 2048 // GT
TS = 256
TPE = CAP // TS
SLOTS = E * CAP
FJ = KF // 2
WCOLS = KD * 2 * F + KF * D
W2AT = KD * 2 * F
PIECE = 512
EPS = 1e-5
CLAMP = 10000.0
DROPPED = 1.0e6
RSQRT_SEED = float(0x5F3759DF)
VSTEP = P + HD


def wait(eng, sem, value):
    if isinstance(value, int) and value <= 0:
        return
    eng.wait_ge(sem, value)


def wait_alone(eng, sem, value, passed):
    eng.wait_ge(sem, value)
    eng.sem_inc(passed, 1)


def mm3(pe, out, a, b, first, last):
    pe.matmul(out, a[0], b[0], start=first, stop=False)
    pe.matmul(out, a[0], b[1], start=False, stop=False)
    return pe.matmul(out, a[1], b[0], start=False, stop=last)


class Memory:

    def __init__(self, nc, ctx, prefix):
        self.nc, self.ctx, self.prefix = nc, ctx, prefix

    def sb(self, name, shape, dt=F32):
        return self.ctx.enter_context(self.nc.sbuf_tensor(self.prefix + name, shape, dt))

    def ps(self, name):
        return self.ctx.enter_context(self.nc.psum_tensor(self.prefix + name, [P, 512], F32))

    def sem(self, name):
        return self.ctx.enter_context(self.nc.semaphore(self.prefix + name))


def inverse_root(dve, y, seed, v):
    dve.tensor_scalar(seed, v.bitcast(I32), 1, None, ALU.logical_shift_right)
    dve.drain()
    dve.tensor_scalar(y.bitcast(I32), seed, -1.0, RSQRT_SEED, ALU.mult, ALU.add)
    dve.drain()
    for _ in range(3):
        s = seed.bitcast(F32)
        dve.tensor_tensor(s, y, y, ALU.mult)
        dve.drain()
        dve.scalar_tensor_tensor(s, s, -0.5, v, ALU.mult, ALU.mult)
        dve.drain()
        dve.scalar_tensor_tensor(y, s, 1.5, y, ALU.add, ALU.mult)
        dve.drain()


class Norm:

    def __init__(self, m, name):
        self.stats = m.sb(name + "_stats", [P, NC, 6])
        self.mv = m.sb(name + "_mv", [P, NC, 2])
        self.var = m.sb(name + "_var", [P, NC])
        self.rstd = m.sb(name + "_rstd", [P, NC])
        self.seed = m.sb(name + "_seed", [P, NC], I32)

    def run(self, dve, src, dst, done):
        for c in range(NC):
            dve.bn_stats(self.stats[:, c, :], src(c))
        dve.drain()
        for c in range(NC):
            dve.bn_aggr(self.mv[:, c, :], self.stats[:, c, :])
        dve.drain()
        dve.tensor_scalar(self.var[:], self.mv[:, :, 1], EPS, None, ALU.add)
        dve.drain()
        inverse_root(dve, self.rstd[:], self.seed[:], self.var[:])
        for c in range(NC):
            ins = dve.tensor_scalar(dst[:, c, :], src(c), self.mv[:, c, 0:1], self.rstd[:, c:c + 1],
                                    ALU.subtract, ALU.mult)
        ins.then_inc(done, 1)


class Router:

    def __init__(self, m, k, bank_a, bank_b, xe):
        self.k, self.bank_a, self.bank_b, self.xe = k, bank_a, bank_b, xe
        self.xnT = m.sb("r_xnT", [P, KD, GT])
        self.lgT = m.sb("r_lgT", [E, GT])
        self.lg = m.sb("r_lg", [P, NC, E])
        self.top = m.sb("r_top", [P, NC, 8])
        self.topi = m.sb("r_topi", [P, NC, 8], U32)
        self.idx = m.sb("r_idx", [P, NC, TOPK])
        self.oh = m.sb("r_oh", [P, NC, TOPK, E])
        self.chosen = m.sb("r_chosen", [P, NC, E], BF16)
        self.diff = m.sb("r_diff", [P, NC])
        self.exp = m.sb("r_exp", [P, NC])
        self.den = m.sb("r_den", [P, NC])
        self.prob = m.sb("r_prob", [P, NC, TOPK])
        self.pos = m.sb("r_pos", [P, NC, E])
        self.ohpos = m.sb("r_ohpos", [P, NC, TOPK, E])
        self.slot = m.sb("r_slot", [P, NC, TOPK])
        self.rank = m.sb("r_rank", [P, NC, TOPK])
        self.keep = m.sb("r_keep", [P, NC, TOPK])
        self.drop = m.sb("r_drop", [P, NC, TOPK])
        self.sslot = m.sb("r_sslot", [P, NC, TOPK])
        self.sidx = m.sb("r_sidx", [P, NC, TOPK], I32)
        self.more = m.sb("r_more", [P, E])
        self.seen = m.sb("r_seen", [P, E], BF16)
        self.xn_ready = m.sem("r_xn_ready")
        self.turned = m.sem("r_turned")
        self.xnT_ready = m.sem("r_xnT_ready")
        self.lgT_made = m.sem("r_lgT_made")
        self.lgT_ready = m.sem("r_lgT_ready")
        self.lg_made = m.sem("r_lg_made")
        self.diff_ready = m.sem("r_diff_ready")
        self.exp_ready = m.sem("r_exp_ready")
        self.chosen_ready = m.sem("r_chosen_ready")
        self.rank_made = m.sem("r_rank_made")
        self.rank_read = m.sem("r_rank_read")
        self.idx_ready = m.sem("r_idx_ready")
        self.scattered = m.sem("r_scattered")
        self.seen_ready = m.sem("r_seen_ready")
        self.count_made = m.sem("r_count_made")

    def start(self, dve):
        dve.memset(self.seen[:], 0.0)
        dve.drain()

    def transposes(self, pe, g, xn):
        pe.wait_ge(self.xn_ready, g + 1)
        for b, bank in enumerate((self.bank_a, self.bank_b)):
            for c in range(2):
                for h in range(KD):
                    at = (h * 2 + c) * P
                    ins = pe.transpose(bank[:, at:at + P], xn[:, 2 * b + c, h * P:(h + 1) * P], self.k.ident[:])
            ins.then_inc(self.turned, 1)

    def keep_xnT(self, act, g):
        for b, bank in enumerate((self.bank_a, self.bank_b)):
            act.wait_ge(self.turned, 2 * g + b + 1)
            act.activation(self.xnT[:, :, b * 2 * P:(b + 1) * 2 * P],
                           bank[:].rearrange("p (h t) -> p h t", h=KD), ACT.Copy).then_inc(self.xnT_ready, 1)

    def logits(self, pe, g):
        pe.wait_ge(self.xnT_ready, 2 * g + 2)
        for h in range(KD):
            ins = pe.matmul(self.bank_a[0:E, :], self.k.wr[:, h, :], self.xnT[:, h, :],
                            start=(h == 0), stop=(h == KD - 1))
        ins.then_inc(self.lgT_made, 1)

    def keep_logits(self, act, g):
        act.wait_ge(self.lgT_made, g + 1)
        act.activation(self.lgT[:], self.bank_a[0:E, :], ACT.Copy).then_inc(self.lgT_ready, 1)

    def turn_logits(self, pe, g):
        pe.wait_ge(self.lgT_ready, g + 1)
        for c in range(NC):
            ins = pe.matmul(self.bank_b[:, c * E:(c + 1) * E], self.lgT[:, c * P:(c + 1) * P],
                            self.k.ident[0:E, 0:E], start=True, stop=True)
        ins.then_inc(self.lg_made, 1)

    def choose(self, dve, g):
        dve.wait_ge(self.lg_made, g + 1)
        dve.tensor_scalar(self.lg[:], self.bank_b[:, 0:NC * E].rearrange("p (c e) -> p c e", c=NC),
                          -CLAMP, CLAMP, ALU.max, ALU.min)
        dve.drain()
        for c in range(NC):
            dve.max(self.top[:, c, :], self.lg[:, c, :])
        dve.drain()
        dve.tensor_tensor(self.diff[:], self.top[:, :, 1], self.top[:, :, 0], ALU.subtract).then_inc(self.diff_ready, 1)
        for c in range(NC):
            dve.max_index(self.topi[:, c, :], self.top[:, c, :], self.lg[:, c, :])
        dve.drain()
        dve.tensor_copy(self.idx[:], self.topi[:, :, 0:TOPK])
        dve.drain()
        dve.tensor_tensor(self.oh[:], self.k.expert[:].unsqueeze(1).unsqueeze(1).broadcast_to([P, NC, TOPK, E]),
                          self.idx[:].unsqueeze(3).broadcast_to([P, NC, TOPK, E]), ALU.is_equal)
        dve.drain()
        dve.tensor_tensor(self.chosen[:], self.oh[:, :, 0, :], self.oh[:, :, 1, :],
                          ALU.add).then_inc(self.chosen_ready, 1)

    def weigh(self, act, g):
        act.wait_ge(self.diff_ready, g + 1)
        act.activation(self.exp[:], self.diff[:], ACT.Exp).then_inc(self.exp_ready, 1)

    def ranks(self, pe, g):
        pe.wait_ge(self.chosen_ready, g + 1)
        wait(pe, self.seen_ready, g + 1)
        out = self.bank_b[:, NC * E:2 * NC * E].rearrange("p (c e) -> p c e", c=NC)
        pe.matmul(out, self.k.before[:], self.chosen[:], start=True, stop=False)
        for c in range(1, NC):
            pe.matmul(out[:, c:NC, :], self.k.ones[:],
                      self.chosen[:, c - 1:c, :].broadcast_to([P, NC - c, E]), start=False, stop=False)
        pe.matmul(out, self.k.ones[:], self.seen[:].unsqueeze(1).broadcast_to([P, NC, E]),
                  start=False, stop=True).then_inc(self.rank_made, 1)

    def place(self, dve, g, wgt, gidx):
        dve.wait_ge(self.rank_made, g + 1)
        dve.tensor_tensor(self.pos[:], self.bank_b[:, NC * E:2 * NC * E].rearrange("p (c e) -> p c e", c=NC),
                          self.k.region[:].unsqueeze(1).broadcast_to([P, NC, E]), ALU.add).then_inc(self.rank_read, 1)
        dve.tensor_reduce(self.more[:], self.chosen[:].rearrange("p c e -> p e c"), AX_X, ALU.add)
        dve.drain()
        dve.tensor_tensor(self.seen[:], self.seen[:], self.more[:], ALU.add).then_inc(self.seen_ready, 1)
        dve.tensor_tensor(self.ohpos[:], self.oh[:], self.pos[:].unsqueeze(2).broadcast_to([P, NC, TOPK, E]), ALU.mult)
        dve.wait_ge(self.exp_ready, g + 1)
        dve.tensor_scalar(self.den[:], self.exp[:], 1.0, 1e-12, ALU.add, ALU.add)
        dve.drain()
        dve.tensor_reduce(self.slot[:], self.ohpos[:], AX_X, ALU.add)
        dve.reciprocal(self.prob[:, :, 0], self.den[:])
        dve.drain()
        dve.scalar_tensor_tensor(self.rank[:], self.idx[:], -float(CAP), self.slot[:], ALU.mult, ALU.add)
        dve.tensor_tensor(self.prob[:, :, 1], self.exp[:], self.prob[:, :, 0], ALU.mult)
        dve.drain()
        dve.tensor_scalar(self.keep[:], self.rank[:], float(CAP), None, ALU.is_lt)
        dve.tensor_scalar(self.drop[:], self.rank[:], float(CAP), DROPPED, ALU.is_ge, ALU.mult)
        dve.drain()
        dve.scalar_tensor_tensor(wgt, self.prob[:], 0.5, self.keep[:], ALU.mult, ALU.mult)
        dve.tensor_tensor(gidx, self.slot[:], self.keep[:], ALU.mult)
        if not (isinstance(g, int) and g == 0):
            dve.wait_ge(self.scattered, 16 * NC * TOPK * g)
        dve.tensor_tensor(self.sidx[:], self.slot[:], self.drop[:], ALU.add).then_inc(self.idx_ready, 1)

    def scatter(self, pool, g, xn):
        pool.wait_ge(self.xn_ready, g + 1)
        wait_alone(pool, self.idx_ready, g + 1, self.k.passed)
        for c in range(NC):
            for j in range(TOPK):
                pool.indirect_dma_start(
                    self.xe, bass.IndirectOffsetOnAxis(ap=self.sidx[:, c, j:j + 1], axis=0), xn[:, c, :], None,
                    bounds_check=SLOTS - 1, oob_is_err=False).then_inc(self.scattered, 16)

    def count(self, pe):
        pe.wait_ge(self.seen_ready, G + 1)
        pe.matmul(self.bank_b[:, 0:E], self.k.ones[:], self.seen[:], start=True, stop=True).then_inc(self.count_made, 1)

    def tiles(self, dve, ntile, first_tile):
        cnt, cnti, scan, zero = self.lg[:, 0, :], self.topi[:, 0, :].bitcast(I32), self.lg[:, 1, :], self.lg[:, 2, :]
        dve.wait_ge(self.count_made, 1)
        dve.tensor_scalar(cnt, self.bank_b[:, 0:E], float(CAP), float(TS - 1), ALU.min, ALU.add)
        dve.memset(zero, 0.0)
        dve.drain()
        dve.tensor_copy(cnti, cnt)
        dve.drain()
        dve.tensor_scalar(cnti, cnti, TS.bit_length() - 1, None, ALU.logical_shift_right)
        dve.drain()
        dve.tensor_scalar(cnt, cnti, 1.0, None, ALU.max)
        dve.drain()
        dve.tensor_copy(ntile[:], cnt)
        dve.tensor_tensor_scan(scan, cnt, zero, 0.0, ALU.add, ALU.add)
        dve.memset(first_tile[:, 0:1], 0.0)
        dve.drain()
        dve.tensor_copy(first_tile[:, 1:E + 1], scan)


def setup_phase(nc, k, inputs):
    with ExitStack() as ctx:
        m = Memory(nc, ctx, "su_")
        raw_qk = m.sb("raw_qk", [P, KD, 2 * D])
        raw_vk = m.sb("raw_vk", [P, KD, 2 * D])
        wc = m.sb("wc", [P, KD, D])
        lt = m.sb("lt", [P, KD, HD])
        low = m.sb("low", [P, P])
        lbd = m.sb("lbd", [P, KD, P])
        bbd = m.sb("bbd", [P, KD, P])
        pb, pm = m.ps("pb"), m.ps("pm")
        loads = m.sem("loads")
        masks0, masks = m.sem("masks0"), m.sem("masks")
        split, tri_ready = m.sem("split"), m.sem("tri_ready")
        bbd_made, bbd_ready, fold_made = m.sem("bbd_made"), m.sem("bbd_ready"), m.sem("fold_made")

        def by_k(w):
            return w.rearrange("(k p) n -> p k n", p=P)

        with nc.Block() as block:
            @block.sync
            def _(sp):
                sp.dma_start(raw_qk[:, :, 0:D], by_k(inputs["wqT"])).then_inc(loads, 16)
                sp.dma_start(raw_qk[:, :, D:2 * D], by_k(inputs["wkT"])).then_inc(loads, 16)
                sp.dma_start(raw_vk[:, :, 0:D], by_k(inputs["wvT"])).then_inc(loads, 16)
                sp.dma_start(raw_vk[:, :, D:2 * D], by_k(inputs["wkT"])).then_inc(loads, 16)
                sp.dma_start(wc[:], by_k(inputs["wcT"])).then_inc(loads, 16)
                sp.dma_start(lt[:], inputs["ltriT"].rearrange("(a h) k e -> (h k) a e", a=KD)).then_inc(loads, 16)
                sp.dma_start(k.wr[:], by_k(inputs["wr"])).then_inc(loads, 16)

            @block.gpsimd
            def _(pool):
                pool.memset(k.ident[:], 0.0)
                pool.memset(k.before[:], 1.0)
                pool.memset(k.causal[:], 1.0)
                pool.memset(k.heads[:], 1.0)
                pool.memset(low[:], 1.0)
                pool.iota(k.expert_i[:], pattern=[[1, E]], base=0, channel_multiplier=0)
                pool.iota(k.region_i[:], pattern=[[CAP, E]], base=0, channel_multiplier=0)
                pool.iota(k.later_i[:], pattern=[[0, GB * 0 + G // GB], [1, GB]], base=0, channel_multiplier=0)
                pool.memset(k.ones[:], 1.0).then_inc(masks0, 1)
                pool.wait_ge(masks0, 1)
                pool.affine_select(out=k.ident[:], in_=k.ident[:], compare_op=ALU.not_equal, fill=1.0,
                                   base=0, pattern=[[-1, P]], channel_multiplier=1)
                pool.affine_select(out=k.before[:], in_=k.before[:], compare_op=ALU.is_ge, fill=0.0,
                                   base=-1, pattern=[[1, P]], channel_multiplier=-1)
                pool.affine_select(out=k.causal[:], in_=k.causal[:], compare_op=ALU.is_ge, fill=0.0,
                                   base=0, pattern=[[1, P]], channel_multiplier=-1)
                pool.affine_select(out=k.heads[:], in_=k.heads[:], compare_op=ALU.is_ge, fill=0.0,
                                   base=0, pattern=[[-HD, HH]], channel_multiplier=1).then_inc(masks0, 1)
                pool.wait_ge(masks0, 2)
                pool.affine_select(out=k.heads[:], in_=k.heads[:], compare_op=ALU.is_ge, fill=0.0,
                                   base=HD - 1, pattern=[[HD, HH]], channel_multiplier=-1).then_inc(masks0, 1)
                pool.wait_ge(masks0, 3)
                pool.tensor_copy(k.same_head[:].rearrange("p (h e) -> p h e", e=HD),
                                 k.heads[:].unsqueeze(2).broadcast_to([P, HH, HD])).then_inc(masks, 1)

            @block.vector
            def _(dve):
                dve.wait_ge(masks, 1)
                dve.wait_ge(masks0, 3)
                dve.tensor_copy(k.expert[:], k.expert_i[:])
                dve.tensor_copy(k.region[:], k.region_i[:])
                dve.tensor_scalar(k.later[:], k.later_i[:].rearrange("p a b -> p (a b)"), 0.5, None, ALU.is_gt)
                dve.tensor_tensor(low[:], k.causal[:], k.same_head[:], ALU.mult)
                dve.drain()
                dve.wait_ge(loads, 16 * 7)
                for a in range(KD):
                    dve.tensor_tensor(lbd[:, a, :].rearrange("p (h e) -> p h e", e=HD),
                                      low[:].rearrange("p (h e) -> p h e", e=HD),
                                      lt[:, a, :].unsqueeze(1).broadcast_to([P, HH, HD]),
                                      ALU.mult).then_inc(tri_ready, 1)
                dve.wait_ge(split, 2)
                dve.tensor_tensor(k.wqk[1][:], raw_qk[:], k.wqk[0][:].bitcast(F32), ALU.subtract)
                dve.tensor_tensor(k.wvk[1][:], raw_vk[:], k.wvk[0][:].bitcast(F32), ALU.subtract)
                dve.wait_ge(split, 3)
                dve.tensor_tensor(k.fold[1][:].rearrange("p a n -> p (a n)"), pm[:],
                                  k.fold[0][:].bitcast(F32).rearrange("p a n -> p (a n)"), ALU.subtract)

            @block.scalar
            def _(act):
                act.wait_ge(loads, 16 * 7)
                act.activation(k.wqk[0][:], raw_qk[:], ACT.Copy).then_inc(split, 1)
                act.activation(k.wvk[0][:], raw_vk[:], ACT.Copy).then_inc(split, 1)
                act.wait_ge(bbd_made, 1)
                act.activation(bbd[:], pb[:, 0:KD * P].rearrange("p (a n) -> p a n", a=KD), ACT.Copy).then_inc(bbd_ready, 1)
                act.wait_ge(fold_made, 1)
                act.activation(k.fold[0][:], pm[:].rearrange("p (a n) -> p a n", a=KD), ACT.Copy).then_inc(split, 1)

            @block.tensor
            def _(pe):
                pe.wait_ge(tri_ready, KD)
                for a in range(KD):
                    ins = pe.matmul(pb[:, a * P:(a + 1) * P], lbd[:, a, :], lbd[:, a, :], start=True, stop=True)
                ins.then_inc(bbd_made, 1)
                pe.wait_ge(bbd_ready, 1)
                for a in range(KD):
                    ins = pe.matmul(pm[:, a * D:(a + 1) * D], bbd[:, a, :], wc[:, a, :], start=True, stop=True)
                ins.then_inc(fold_made, 1)


def route_phase(nc, k, x_in, xe, ye, experts, w, route_out):
    wgt, gidx, ntile, first_tile = route_out
    with ExitStack() as ctx:
        m = Memory(nc, ctx, "r1_")
        xin = m.sb("xin", [P, 2, NC, D])
        xn = [m.sb(f"xn{s}", [P, NC, D]) for s in range(2)]
        zeros = m.sb("zeros", [P, D])
        raw = m.sb("raw", [P, WCOLS])
        banks = [m.ps(f"bank{i}") for i in range(4)]
        r = Router(m, k, banks[0], banks[1], xe)
        r2 = banks[2:4]
        norm = Norm(m, "n")
        x_loaded = [m.sem(f"x_loaded{s}") for s in range(2)]
        raw_loaded, w_high, w_low = m.sem("raw_loaded"), m.sem("w_high"), m.sem("w_low")
        zeroed, ye_clear = m.sem("zeroed"), m.sem("ye_clear")

        x_g = x_in.rearrange("(g c p) d -> g p c d", p=P, c=NC)
        FILL = GT
        fills = CAP // FILL
        xe_clear = [m.sem(f"xe_clear{f}") for f in range(fills)]

        def clear(q, dst, f, sem):
            rows = dst.rearrange("(e f p r) d -> f e p r d", e=E, f=fills, p=P, r=FILL // P)
            for e in range(E):
                q.dma_start(rows[f, e], zeros[:].unsqueeze(1).broadcast_to([P, FILL // P, D])).then_inc(sem, 16)

        with nc.Block() as block:
            @block.sync
            def _(sp):
                load_expert(sp, w, 0, raw, raw_loaded)

                def load(g, s):
                    sp.dma_start(xin[:, s, :, :], x_g[bass.ds(g, 1)].rearrange("o p c d -> p (o c) d")
                                 if not isinstance(g, int) else x_g[g]).then_inc(x_loaded[s], 16)

                load(0, 0)
                load(1, 1)
                with sp.Fori(0, G // 2 - 1) as i:
                    for s in range(2):
                        sp.wait_ge(r.xn_ready, 2 * i + s + 1)
                        load(2 * i + s + 2, s)

            @block.scalar
            def _(act):
                act.wait_ge(zeroed, 1)
                for f in range(fills):
                    clear(act, xe, f, xe_clear[f])
                clear_region(act, ye, 0, zeros, ye_clear)
                act_copy_high(act, experts[0], raw, raw_loaded, w_high)

                def step(g):
                    r.keep_xnT(act, g)
                    r.keep_logits(act, g)
                    r.weigh(act, g)

                with act.Fori(0, G) as g:
                    step(g)
                act.wait_ge(ye_clear, 16)

            @block.vector
            def _(dve):
                dve.memset(zeros[:], 0.0).then_inc(zeroed, 1)
                r.start(dve)
                dve.nop().then_inc(r.seen_ready, 1)

                def ln(g, s, i):
                    dve.wait_ge(x_loaded[s], 16 * (i + 1))
                    if not (isinstance(g, int) and g < 2):
                        dve.wait_ge(r.scattered, 16 * NC * TOPK * (g - 1))
                    norm.run(dve, lambda c: xin[:, s, c, :], xn[s], r.xn_ready)

                def finish(g):
                    r.choose(dve, g)
                    r.place(dve, g, at_group(wgt, g), at_group(gidx, g))

                ln(0, 0, 0)
                ln(1, 1, 0)
                finish(0)
                with dve.Fori(1, G // 2) as i:
                    ln(2 * i, 0, i)
                    finish(2 * i - 1)
                    ln(2 * i + 1, 1, i)
                    finish(2 * i)
                finish(G - 1)
                r.tiles(dve, ntile, first_tile)

            @block.gpsimd
            def _(pool):
                pool_split_low(pool, experts[0], raw, w_high, w_low)
                for i in range(fills):
                    pool.wait_ge(xe_clear[i], 16 * E)
                    r.scatter(pool, i, xn[i % 2])
                r.scatter(pool, fills, xn[fills % 2])
                with pool.Fori(fills // 2 + 1, G // 2) as i:
                    for s in range(2):
                        r.scatter(pool, 2 * i + s, xn[s])
                pool.wait_ge(r.scattered, 16 * NC * TOPK * G)

            @block.tensor
            def _(pe):
                def step(g, s):
                    if not (isinstance(g, int) and g == 0):
                        pe.wait_ge(r.rank_read, g)
                    r.transposes(pe, g, xn[s])
                    r.logits(pe, g)
                    r.turn_logits(pe, g)
                    r.ranks(pe, g)

                step(0, 0)
                step(1, 1)
                with pe.Fori(1, G // 2) as i:
                    for s in range(2):
                        step(2 * i + s, s)
                r.count(pe)


def at_group(t, g):
    return t[:, g] if isinstance(g, int) else t[:, bass.ds(g, 1)].rearrange("p o c j -> p (o c) j")


def load_expert(q, w, e, raw, sem):
    w1, w3, w2 = w
    pick = (lambda t: t[e]) if isinstance(e, int) else (lambda t: t[bass.ds(e, 1)].rearrange("o a b -> (o a) b"))
    w13 = raw[:, 0:W2AT].rearrange("p (k n) -> p k n", k=KD)
    q.dma_start(w13[:, :, 0:F], pick(w1).rearrange("(k p) f -> p k f", p=P)).then_inc(sem, 16)
    q.dma_start(w13[:, :, F:2 * F], pick(w3).rearrange("(k p) f -> p k f", p=P)).then_inc(sem, 16)
    q.dma_start(raw[:, W2AT:WCOLS].rearrange("p (k d) -> p k d", k=KF),
                pick(w2).rearrange("(k p) d -> p k d", p=P)).then_inc(sem, 16)


def act_copy_high(act, pair, raw, raw_loaded, w_high):
    act.wait_ge(raw_loaded, 48)
    act.activation(pair[0][:], raw[:], ACT.Copy).then_inc(w_high, 1)


def pool_split_low(pool, pair, raw, w_high, w_low):
    pool.wait_ge(w_high, 1)
    pool.tensor_tensor(pair[1][:], raw[:], pair[0][:].bitcast(F32), ALU.subtract).then_inc(w_low, 1)
    pool.wait_ge(w_low, 1)


def clear_region(q, ye, e, zeros, sem):
    rows = ye.rearrange("(e p r) d -> e p r d", e=E + 1, p=P)
    region = rows[e] if isinstance(e, int) else rows[bass.ds(e, 1)].rearrange("o p r d -> (o p) r d")
    q.dma_start(region, zeros[:].unsqueeze(1).broadcast_to([P, CAP // P, D])).then_inc(sem, 16)


def expert_phase(nc, k, name, xe, ye, slot_a, w, route_out, clear):
    _, _, ntile, first_tile = route_out
    with ExitStack() as ctx:
        m = Memory(nc, ctx, name)
        slot_b = [m.sb("wb_hi", [P, WCOLS], F32R), m.sb("wb_lo", [P, WCOLS], F32R)]
        slots = [slot_a, slot_b]
        raw = m.sb("raw", [P, WCOLS])
        xrow = m.sb("xrow", [P, 2, D])
        xT = [m.sb("xT_hi", [P, KD, TS], F32R), m.sb("xT_lo", [P, KD, TS], F32R)]
        gate = m.sb("gate", [P, 2, 512])
        hid = m.sb("hid", [P, 2, 512])
        h = [m.sb("h_hi", [P, KF * TS], F32R), m.sb("h_lo", [P, KF * TS], F32R)]
        yrow = m.sb("yrow", [P, 2, D])
        prime = m.sb("prime", [P, KD, E])
        zeros = m.sb("zeros", [P, D])
        ps1 = [m.ps(f"ps1_{b}") for b in range(2)]
        ps3 = [m.ps(f"ps3_{b}") for b in range(2)]
        psx = m.ps("psx")
        psy = m.ctx.enter_context(nc.psum_tensor(name + "psy", [P, 2, 512], F32))

        x_loaded = m.sem("x_loaded")
        x_turned = m.sem("x_turned")
        x_high = m.sem("x_high")
        x_ready = m.sem("x_ready")
        h_made = m.sem("h_made")
        gated = m.sem("gated")
        hid_ready = m.sem("hid_ready")
        h_high = m.sem("h_high")
        h_ready = m.sem("h_ready")
        y_made = m.sem("y_made")
        y_kept = m.sem("y_kept")
        y_stored = m.sem("y_stored")
        zeroed = m.sem("zeroed")
        cleared = m.sem("cleared")
        raw_loaded = m.sem("raw_loaded")
        w_low = m.sem("w_low")
        w_high = m.sem("w_high")
        w_ready = m.sem("w_ready")

        w_prime = k.wr_dram.rearrange("(k p) n -> p k n", p=P)
        xe_t = xe.rearrange("(n s p) d -> n p s d", s=2, p=P)
        ye_t = ye.rearrange("(n s p) d -> n p s d", s=2, p=P)

        def tile_of(t, i):
            return t[bass.ds(i, 1)].rearrange("o p s d -> p (o s) d")

        def experts(eng, body, tile_body, want_tiles=True):
            with eng.Fori(0, E // 2) as i:
                for s in range(2):
                    e = i * 2 + s
                    f = eng.value_load(first_tile[0:1, bass.ds(e, 1)], min_val=0, max_val=E * TPE)
                    body(e, s, f)
                    if want_tiles:
                        n = eng.value_load(ntile[0:1, bass.ds(e, 1)], min_val=1, max_val=TPE)
                        with eng.Fori(0, n) as t:
                            tile_body(e, s, t, eng.snap(f + t))

        def following(e, s):
            return e + 1 if s == 0 else (e + 1) % E

        def total(eng):
            return eng.value_load(first_tile[0:1, E:E + 1], min_val=E, max_val=E * TPE)

        with nc.Block() as block:
            @block.sync
            def _(sp):
                def expert(e, s, f):
                    sp.wait_ge(w_ready, e + 1)
                    load_expert(sp, w, following(e, s), raw, raw_loaded)
                    if clear:
                        sp.wait_ge(cleared, 16 * e + 16)
                        clear_region(sp, ye, e + 1, zeros, cleared)

                def tile(e, s, t, g):
                    sp.wait_ge(x_turned, g + 1)
                    sp.dma_start(xrow[:], tile_of(xe_t, e * TPE + t)).then_inc(x_loaded, 16)

                if clear:
                    sp.wait_ge(zeroed, 1)
                    clear_region(sp, ye, E, zeros, cleared)
                experts(sp, expert, tile)
                if clear:
                    sp.wait_ge(cleared, 16 * (E + 1))
                sp.wait_ge(x_turned, total(sp) + 1)
                sp.dma_start(xrow[:], xe_t[0]).then_inc(x_loaded, 16)


            @block.gpsimd
            def _(pool):
                pool.nop().then_inc(w_ready, 1)

                def expert(e, s, f):
                    dst = slots[1 - s]
                    with pool.Fori(0, WCOLS // PIECE) as q:
                        pool.wait_ge(raw_loaded, 48 * e + 48)
                        pool.wait_ge(y_made, f + 1)
                        at = q * PIECE
                        pool.tensor_copy(dst[0][:, bass.ds(at, PIECE)], raw[:, bass.ds(at, PIECE)]).then_inc(w_high, 1)
                        pool.wait_ge(w_high, e * (WCOLS // PIECE) + q + 1)
                        pool.tensor_tensor(dst[1][:, bass.ds(at, PIECE)], raw[:, bass.ds(at, PIECE)],
                                           dst[0][:, bass.ds(at, PIECE)].bitcast(F32), ALU.subtract).then_inc(w_low, 1)
                    pool.wait_ge(w_low, (e + 1) * (WCOLS // PIECE))
                    pool.nop().then_inc(w_ready, 1)

                experts(pool, expert, None, want_tiles=False)

            @block.tensor
            def _(pe):
                pe.nop().then_inc(x_turned, 1)
                pe.nop().then_inc(y_made, 1)

                def turn(n_loaded):
                    pe.wait_ge(x_loaded, n_loaded)
                    for half in range(KD):
                        for sub in range(2):
                            at = half * TS + sub * P
                            ins = pe.transpose(psx[:, at:at + P], xrow[:, sub, half * P:(half + 1) * P], k.ident[:])
                    ins.then_inc(x_turned, 1)

                def expert(e, s, f):
                    pe.wait_ge(w_ready, e + 1)

                def tile(e, s, t, g):
                    hi, lo = slots[s]

                    def wt(at):
                        return hi[:, at:at + P], lo[:, at:at + P]

                    def w2t(f):
                        at = W2AT + f * D
                        return hi[:, at:at + D], lo[:, at:at + D]

                    pe.wait_ge(x_ready, g + 1)
                    for j in range(FJ):
                        pe.wait_ge(hid_ready, 4 * g + j + 1)
                        for fi in range(2):
                            f = 2 * j + fi
                            for ps, base in ((ps1[j % 2], 0), (ps3[j % 2], F)):
                                for kk in range(KD):
                                    ins = mm3(pe, ps[:, fi * TS:(fi + 1) * TS], wt(kk * 2 * F + base + f * P),
                                              (xT[0][:, kk, :], xT[1][:, kk, :]), kk == 0, kk == KD - 1)
                        ins.then_inc(h_made, 1)
                    turn(16 * g + 32)
                    pe.wait_ge(y_kept, g + 1)
                    for j in range(FJ):
                        pe.wait_ge(h_ready, 4 * g + j + 1)
                        for fi in range(2):
                            f = 2 * j + fi
                            for sub in range(2):
                                at = f * TS + sub * P
                                ins = mm3(pe, psy[:, sub, 0:D], (h[0][:, at:at + P], h[1][:, at:at + P]), w2t(f),
                                          f == 0, f == KF - 1)
                    ins.then_inc(y_made, 1)

                turn(16)
                experts(pe, expert, tile)

            @block.scalar
            def _(act):
                act.nop().then_inc(y_kept, 1)
                act.dma_start(prime[:], w_prime).then_inc(y_stored, 16)

                def high_x(n):
                    act.wait_ge(x_turned, n)
                    act.activation(xT[0][:], psx[:].rearrange("p (k t) -> p k t", k=KD), ACT.Copy).then_inc(x_high, 1)

                def tile(e, s, t, g):
                    for j in range(FJ):
                        act.wait_ge(h_made, 4 * g + j + 1)
                        act.wait_ge(hid_ready, 4 * g + j + 1)
                        act.activation(gate[:, j % 2, :], ps1[j % 2][:], ACT.Silu).then_inc(gated, 1)
                        act.wait_ge(hid_ready, 4 * g + j + 3)
                        act.activation(h[0][:, j * 512:(j + 1) * 512], hid[:, j % 2, :], ACT.Copy).then_inc(h_high, 1)
                    high_x(g + 3)
                    act.wait_ge(y_made, g + 2)
                    act.wait_ge(y_stored, 16 * g + 16)
                    act.activation(yrow[:], psy[:, :, 0:D], ACT.Copy).then_inc(y_kept, 1)
                    if clear:
                        act.wait_ge(cleared, 16 * e + 16)
                    act.wait_ge(y_kept, g + 2)
                    act.dma_start(tile_of(ye_t, e * TPE + t), yrow[:]).then_inc(y_stored, 16)

                high_x(2)
                experts(act, lambda e, s, f: None, tile)
                wait_alone(act, y_stored, 16 * total(act) + 16, k.passed)

            @block.vector
            def _(dve):
                dve.memset(zeros[:], 0.0).then_inc(zeroed, 1)
                dve.nop().then_inc(hid_ready, 2)

                def low_x(n):
                    dve.wait_ge(x_high, n)
                    dve.tensor_tensor(xT[1][:], psx[:].rearrange("p (k t) -> p k t", k=KD), xT[0][:].bitcast(F32),
                                      ALU.subtract).then_inc(x_ready, 1)

                def tile(e, s, t, g):
                    for j in range(FJ):
                        dve.wait_ge(gated, 4 * g + j + 1)
                        dve.tensor_tensor(hid[:, j % 2, :], ps3[j % 2][:], gate[:, j % 2, :],
                                          ALU.mult).then_inc(hid_ready, 1)
                        dve.wait_ge(h_high, 4 * g + j + 1)
                        at = slice(j * 512, (j + 1) * 512)
                        dve.tensor_tensor(h[1][:, at], hid[:, j % 2, :], h[0][:, at].bitcast(F32),
                                          ALU.subtract).then_inc(h_ready, 1)
                    low_x(g + 2)

                low_x(1)
                experts(dve, lambda e, s, f: None, tile)


def middle_phase(nc, k, x_in, x2_out, xe, ye, route_in, route_out):
    wgt_in, gidx_in, _, _ = route_in
    wgt_out, gidx_out, ntile, first_tile = route_out
    with ExitStack() as ctx:
        m = Memory(nc, ctx, "mi_")
        x1 = m.sb("x1", [P, 2, NC, D])
        yg = m.sb("yg", [P, NC, TOPK, D])
        gi = m.sb("gi", [P, NC, TOPK], I32)
        xn = m.sb("xn", [P, NC, D])
        xT = [m.sb("xT_hi", [P, KD, GT], F32R), m.sb("xT_lo", [P, KD, GT], F32R)]
        qT = m.sb("qT", [P, KD, GT])
        kT = m.sb("kT", [P, KD, GT])
        qx = m.sb("qx", [P, KD, HH, GT])
        vpad = [m.sb(f"vpad{b}", [P, KD * HH * P + P]) for b in range(2)]
        kt = [m.sb(f"kt{b}", [P, D]) for b in range(2)]
        prob = [m.sb(f"prob{b}", [P, H, P]) for b in range(2)]
        state = [m.sb(f"state{b}", [P, KD, P]) for b in range(2)]
        update = m.sb("update", [P, KD, P])
        yT = [m.sb("yT_hi", [P, KD, P], F32R), m.sb("yT_lo", [P, KD, P], F32R)]
        x2 = m.sb("x2", [P, NC, D])
        xn2 = m.sb("xn2", [P, NC, D])
        sc = [m.ps("sc0"), m.ps("sc1")]
        wide = [m.ps("wide0"), m.ps("wide1")]
        vk, yt, kv, op = m.ps("vk"), m.ps("yt"), m.ps("kv"), m.ps("op")
        norm1, norm2 = Norm(m, "n1"), Norm(m, "n2")
        r = Router(m, k, wide[0], wide[1], xe)

        x_loaded = m.sem("x_loaded")
        gi_ready = m.sem("gi_ready")
        gathered = m.sem("gathered")
        combined = m.sem("combined")
        xn_ready = m.sem("xn_ready")
        turned = m.sem("turned")
        x_high = m.sem("x_high")
        xT_ready = m.sem("xT_ready")
        qk_made = m.sem("qk_made")
        qk_kept = m.sem("qk_kept")
        qx_ready = m.sem("qx_ready")
        vk_made = m.sem("vk_made")
        vk_kept = m.sem("vk_kept")
        sc_made = m.sem("sc_made")
        prob_ready = m.sem("prob_ready")
        kv_made = m.sem("kv_made")
        state_ready = m.sem("state_ready")
        fresh = m.sem("fresh")
        y_made = m.sem("y_made")
        y_high = m.sem("y_high")
        y_ready = m.sem("y_ready")
        o_made = m.sem("o_made")
        x2_ready = m.sem("x2_ready")
        x2_stored = m.sem("x2_stored")
        vzero = m.sem("vzero")

        x_g = x_in.rearrange("(g c p) d -> g p c d", p=P, c=NC)
        x2_g = x2_out.rearrange("(g c p) d -> g p c d", p=P, c=NC)

        def group(t, g):
            return t[g] if isinstance(g, int) else t[bass.ds(g, 1)].rearrange("o p c d -> p (o c) d")

        def slot(g):
            return g % 2

        def x1_of(g, c):
            s = slot(g)
            return x1[:, s, c, :] if isinstance(s, int) else x1[:, bass.ds(s, 1), c, :].rearrange("p o d -> p (o d)")

        def rounds(eng, step):
            step(0, True, False)
            step(1, False, False)
            with eng.Fori(2, G - 1) as g:
                step(g, False, False)
            step(G - 1, False, True)

        with nc.Block() as block:
            @block.sync
            def _(sp):
                def load(g):
                    s = slot(g)
                    dst = x1[:, s] if isinstance(s, int) else x1[:, bass.ds(s, 1)].rearrange("p o c d -> p (o c) d")
                    sp.dma_start(dst, group(x_g, g)).then_inc(x_loaded, 16)

                def step(g, first, last):
                    if not last:
                        wait_alone(sp, combined, g + 1, k.passed)
                        wait(sp, x2_ready, NC * g)
                        load(g + 1)
                    sp.wait_ge(x2_ready, NC * g + NC)
                    sp.dma_start(group(x2_g, g), x2[:]).then_inc(x2_stored, 16)

                load(0)
                rounds(sp, step)
                sp.wait_ge(x2_stored, 16 * G)

            @block.gpsimd
            def _(pool):
                pool.memset(vpad[0][:], 0.0).then_inc(vzero, 1)
                pool.memset(vpad[1][:], 0.0).then_inc(vzero, 1)

                def gather(g):
                    wait(pool, combined, g)
                    pool.tensor_copy(gi[:], at_group(gidx_in, g)).then_inc(gi_ready, 1)
                    wait_alone(pool, gi_ready, g + 1, k.passed)
                    for c in range(NC):
                        for j in range(TOPK):
                            pool.indirect_dma_start(
                                yg[:, c, j, :], None, ye[0:SLOTS, :],
                                bass.IndirectOffsetOnAxis(ap=gi[:, c, j:j + 1], axis=0),
                                bounds_check=SLOTS - 1, oob_is_err=False).then_inc(gathered, 16)

                def step(g, first, last):
                    if not last:
                        gather(g + 1)
                    if not first:
                        r.scatter(pool, g - 1, xn2)

                gather(0)
                rounds(pool, step)
                r.scatter(pool, G - 1, xn2)
                pool.wait_ge(r.scattered, 16 * NC * TOPK * G)

            @block.tensor
            def _(pe):
                def values(c):
                    pass

                def turn(g):
                    pe.wait_ge(xn_ready, g + 1)
                    for b in range(2):
                        for c in range(2):
                            for h in range(KD):
                                at = (h * 2 + c) * P
                                ins = pe.transpose(wide[b][:, at:at + P], xn[:, 2 * b + c, h * P:(h + 1) * P], k.ident[:])
                        ins.then_inc(turned, 1)

                def project_qk(g):
                    pe.wait_ge(xT_ready, 2 * g + 2)
                    for n in range(2 * KD):
                        if n >= 2:
                            pe.wait_ge(qk_kept, 2 * KD * g + n - 1)
                        for kk in range(KD):
                            cols = slice(n * P, (n + 1) * P)
                            ins = mm3(pe, wide[n % 2][:], (k.wqk[0][:, kk, cols], k.wqk[1][:, kk, cols]),
                                      (xT[0][:, kk, :], xT[1][:, kk, :]), kk == 0, kk == KD - 1)
                        ins.then_inc(qk_made, 1)

                def project_vk(g, c):
                    wait(pe, vk_kept, 2 * (NC * g + c))
                    rows = slice(c * P, (c + 1) * P)
                    for kk in range(KD):
                        ins = mm3(pe, vk[:], (xT[0][:, kk, rows], xT[1][:, kk, rows]),
                                  (k.wvk[0][:, kk, :], k.wvk[1][:, kk, :]), kk == 0, kk == KD - 1)
                    ins.then_inc(vk_made, 1)

                def scores(g, c):
                    for q in range(4):
                        half, u = q // 2, 16 * g + 4 * c + q
                        if c == 0:
                            pe.wait_ge(qk_kept, 2 * KD * g + KD + half + 1)
                            pe.wait_ge(qx_ready, KD * g + half + 1)
                        wait(pe, prob_ready, u - 1)
                        pe.matmul(sc[q % 2][:], kT[:, half, c * P:(c + 1) * P],
                                  qx[:, half, (q % 2) * 4:(q % 2) * 4 + 4, c * P:(c + 1) * P],
                                  start=True, stop=True).then_inc(sc_made, 1)

                def vdiag(c, half):
                    at = half * HH * P
                    return vpad[c % 2][:, at:at + HH * VSTEP].rearrange("p (h x) -> p h x", x=VSTEP)[:, :, 0:HD]

                def update_state(g, c):
                    pe.wait_ge(vk_kept, 2 * (NC * g + c + 1))
                    wait(pe, state_ready, NC * g + c)
                    for half in range(KD):
                        ins = pe.matmul(kv[:, half * P:(half + 1) * P], kt[c % 2][:, half * P:(half + 1) * P],
                                        vdiag(c, half), start=True, stop=True)
                    ins.then_inc(kv_made, 1)

                def attend(g, c):
                    wait(pe, state_ready, NC * g + c)
                    if c == 0:
                        pe.wait_ge(fresh, g + 1)
                    wait(pe, y_ready, NC * g + c)
                    for half in range(KD):
                        out = yt[:, half * P:(half + 1) * P]
                        pe.matmul(out, state[c % 2][:, half, :], qT[:, half, c * P:(c + 1) * P], start=True, stop=False)
                        for hh in range(HH):
                            h = half * HH + hh
                            if hh % 4 == 0:
                                pe.wait_ge(prob_ready, 16 * g + 4 * c + h // 4 + 1)
                            ins = pe.matmul(out, vpad[c % 2][:, h * P:(h + 1) * P], prob[c % 2][:, h, :],
                                            start=False, stop=(hh == HH - 1))
                        ins.then_inc(y_made, 1)

                def project_out(g, c):
                    pe.wait_ge(y_ready, NC * g + c + 1)
                    wait(pe, x2_ready, NC * g + c)
                    for half in range(KD):
                        ins = mm3(pe, op[:, 0:D], (yT[0][:, half, :], yT[1][:, half, :]),
                                  (k.fold[0][:, half, :], k.fold[1][:, half, :]), half == 0, half == KD - 1)
                    ins.then_inc(o_made, 1)

                def step(g, first, last):
                    turn(g)
                    project_qk(g)
                    project_vk(g, 0)
                    scores(g, 0)
                    for c in range(NC):
                        update_state(g, c)
                        if c == 3 and not first:
                            r.ranks(pe, g - 1)
                        attend(g, c)
                        if c < NC - 1:
                            project_vk(g, c + 1)
                            scores(g, c + 1)
                        project_out(g, c)
                        if not first and c == 0:
                            pe.wait_ge(qk_kept, 2 * KD * g + 2 * KD)
                            r.transposes(pe, g - 1, xn2)
                        if not first and c == 1:
                            r.logits(pe, g - 1)
                        if not first and c == 2:
                            r.turn_logits(pe, g - 1)
                    if not first:
                        pe.wait_ge(r.rank_read, g)

                rounds(pe, step)
                r.transposes(pe, G - 1, xn2)
                r.logits(pe, G - 1)
                r.turn_logits(pe, G - 1)
                r.ranks(pe, G - 1)
                pe.wait_ge(r.rank_read, G)
                r.count(pe)

            @block.scalar
            def _(act):
                def keep_vk(g, c):
                    act.wait_ge(vk_made, NC * g + c + 1)
                    wait(act, y_made, KD * (NC * g + c - 1))
                    dst = vpad[c % 2]
                    for half in range(KD):
                        at = half * HH * P
                        ins = act.activation(
                            dst[:, at:at + HH * VSTEP].rearrange("p (h x) -> p h x", x=VSTEP)[:, :, 0:HD],
                            vk[:, half * P:(half + 1) * P].rearrange("p (h e) -> p h e", e=HD), ACT.Copy)
                    ins.then_inc(vk_kept, 1)
                    act.activation(kt[c % 2][:], vk[:, D:2 * D], ACT.Copy).then_inc(vk_kept, 1)

                def step(g, first, last):
                    for b in range(2):
                        act.wait_ge(turned, 2 * g + b + 1)
                        act.activation(xT[0][:, :, b * 2 * P:(b + 1) * 2 * P],
                                       wide[b][:].rearrange("p (h t) -> p h t", h=KD), ACT.Copy).then_inc(x_high, 1)
                    for n in range(2 * KD):
                        act.wait_ge(qk_made, 2 * KD * g + n + 1)
                        dst = (qT, kT)[n // KD]
                        act.activation(dst[:, n % KD, :], wide[n % 2][:], ACT.Copy).then_inc(qk_kept, 1)
                    keep_vk(g, 0)
                    for c in range(NC):
                        act.wait_ge(y_made, KD * (NC * g + c + 1))
                        wait(act, o_made, NC * g + c)
                        act.activation(yT[0][:], yt[:, 0:KD * P].rearrange("p (a t) -> p a t", a=KD),
                                       ACT.Copy).then_inc(y_high, 1)
                        if c < NC - 1:
                            keep_vk(g, c + 1)
                        if not first and c == 0:
                            r.keep_xnT(act, g - 1)
                        if not first and c == 1:
                            r.keep_logits(act, g - 1)
                        if not first and c == 2:
                            r.weigh(act, g - 1)

                act.wait_ge(vzero, 2)
                rounds(act, step)
                r.keep_xnT(act, G - 1)
                r.keep_logits(act, G - 1)
                r.weigh(act, G - 1)

            @block.vector
            def _(dve):
                def combine(g):
                    dve.wait_ge(x_loaded, 16 * g + 16)
                    dve.wait_ge(gathered, 16 * NC * TOPK * (g + 1))
                    w = at_group(wgt_in, g)
                    for j in range(TOPK):
                        for c in range(NC):
                            ins = dve.scalar_tensor_tensor(x1_of(g, c), yg[:, c, j, :], w[:, c, j:j + 1], x1_of(g, c),
                                                           ALU.mult, ALU.add)
                        if j == 0:
                            dve.drain()
                    ins.then_inc(combined, 1)

                def set_out(g):
                    for half in range(KD):
                        dve.wait_ge(qk_kept, 2 * KD * g + half + 1)
                        for hh in range(HH):
                            ins = dve.tensor_scalar(qx[:, half, hh, :], qT[:, half, :], k.heads[:, hh:hh + 1], None, ALU.mult)
                        ins.then_inc(qx_ready, 1)

                def mask(g, c):
                    wait(dve, y_made, KD * (NC * g + c - 1))
                    for q in range(4):
                        dve.wait_ge(sc_made, 16 * g + 4 * c + q + 1)
                        dve.tensor_tensor(prob[c % 2][:, 4 * q:4 * q + 4, :],
                                          sc[q % 2][:].rearrange("p (h t) -> p h t", h=4),
                                          k.causal[:].unsqueeze(1).broadcast_to([P, 4, P]), ALU.mult).then_inc(prob_ready, 1)

                def advance(g, c):
                    dve.wait_ge(kv_made, NC * g + c + 1)
                    dve.tensor_tensor(update[:], kv[:, 0:KD * P].rearrange("p (a t) -> p a t", a=KD),
                                      k.same_head[:].unsqueeze(1).broadcast_to([P, KD, P]), ALU.mult)
                    dve.drain()
                    wait(dve, y_made, KD * (NC * g + c))
                    dve.tensor_tensor(state[(c + 1) % 2][:], state[c % 2][:], update[:], ALU.add).then_inc(state_ready, 1)

                def low_y(g, c):
                    dve.wait_ge(y_high, NC * g + c + 1)
                    dve.tensor_tensor(yT[1][:], yt[:, 0:KD * P].rearrange("p (a t) -> p a t", a=KD),
                                      yT[0][:].bitcast(F32), ALU.subtract).then_inc(y_ready, 1)

                def add_out(g, c):
                    dve.wait_ge(o_made, NC * g + c + 1)
                    if c == 0:
                        wait(dve, x2_stored, 16 * g)
                    dve.tensor_tensor(x2[:, c, :], op[:, 0:D], x1_of(g, c), ALU.add).then_inc(x2_ready, 1)

                def place(g):
                    r.place(dve, g, at_group(wgt_out, g), at_group(gidx_out, g))

                def step(g, first, last):
                    for b in range(2):
                        dve.wait_ge(x_high, 2 * g + b + 1)
                        cols = slice(b * 2 * P, (b + 1) * 2 * P)
                        dve.tensor_tensor(xT[1][:, :, cols], wide[b][:].rearrange("p (h t) -> p h t", h=KD),
                                          xT[0][:, :, cols].bitcast(F32), ALU.subtract).then_inc(xT_ready, 1)
                    at = slice(g, g + 1) if isinstance(g, int) else bass.ds(g, 1)
                    dve.tensor_scalar(state[0][:], state[0][:], k.later[:, at], None, ALU.mult).then_inc(fresh, 1)
                    set_out(g)
                    mask(g, 0)
                    if not first:
                        normed2(g)
                    for c in range(NC):
                        advance(g, c)
                        if c == 3 and not first:
                            place(g - 1)
                        low_y(g, c)
                        if c < NC - 1:
                            mask(g, c + 1)
                        add_out(g, c)
                        if c == 0 and not last:
                            combine(g + 1)
                        if c == 1 and not last:
                            norm1.run(dve, lambda cc: x1_of(g + 1, cc), xn, xn_ready)
                        if c == 2 and not first:
                            r.choose(dve, g - 1)

                def normed2(g):
                    dve.wait_ge(x2_ready, NC * g)
                    if not (isinstance(g, int) and g < 2):
                        dve.wait_ge(r.scattered, 16 * NC * TOPK * (g - 1))
                    norm2.run(dve, lambda c: x2[:, c, :], xn2, r.xn_ready)

                dve.memset(state[0][:], 0.0)
                dve.nop().then_inc(r.seen_ready, 1)
                r.start(dve)
                combine(0)
                dve.drain()
                norm1.run(dve, lambda cc: x1_of(0, cc), xn, xn_ready)
                rounds(dve, step)
                normed2(G)
                r.choose(dve, G - 1)
                place(G - 1)
                r.tiles(dve, ntile, first_tile)


def final_phase(nc, k, x2_in, ye, out, route_in):
    wgt, gidx, _, _ = route_in
    with ExitStack() as ctx:
        m = Memory(nc, ctx, "fi_")
        x = [m.sb(f"x{s}", [P, NC, D]) for s in range(2)]
        yg = [m.sb(f"yg{s}", [P, NC, TOPK, D]) for s in range(2)]
        gi = [m.sb(f"gi{s}", [P, NC, TOPK], I32) for s in range(2)]
        x_loaded = [m.sem(f"x_loaded{s}") for s in range(2)]
        gi_ready = m.sem("gi_ready")
        gathered = [m.sem(f"gathered{s}") for s in range(2)]
        added = m.sem("added")
        stored = [m.sem(f"stored{s}") for s in range(2)]

        x_g = x2_in.rearrange("(g c p) d -> g p c d", p=P, c=NC)
        out_g = out.rearrange("(g c p) d -> g p c d", p=P, c=NC)

        def group(t, g):
            return t[g] if isinstance(g, int) else t[bass.ds(g, 1)].rearrange("o p c d -> p (o c) d")

        def rounds(eng, step):
            for s in range(2):
                step(s, s, 0)
            with eng.Fori(1, G // 2) as i:
                for s in range(2):
                    step(2 * i + s, s, i)

        with nc.Block() as block:
            @block.sync
            def _(sp):
                def step(g, s, i):
                    wait(sp, stored[s], 16 * i)
                    sp.dma_start(x[s][:], group(x_g, g)).then_inc(x_loaded[s], 16)

                rounds(sp, step)

            @block.gpsimd
            def _(pool):
                def step(g, s, i):
                    if not (isinstance(g, int) and g < 2):
                        pool.wait_ge(added, g - 1)
                    pool.tensor_copy(gi[s][:], at_group(gidx, g)).then_inc(gi_ready, 1)
                    wait_alone(pool, gi_ready, g + 1, k.passed)
                    for c in range(NC):
                        for j in range(TOPK):
                            pool.indirect_dma_start(
                                yg[s][:, c, j, :], None, ye[0:SLOTS, :],
                                bass.IndirectOffsetOnAxis(ap=gi[s][:, c, j:j + 1], axis=0),
                                bounds_check=SLOTS - 1, oob_is_err=False).then_inc(gathered[s], 16)

                rounds(pool, step)

            @block.vector
            def _(dve):
                def step(g, s, i):
                    dve.wait_ge(x_loaded[s], 16 * i + 16)
                    dve.wait_ge(gathered[s], 16 * NC * TOPK * (i + 1))
                    w = at_group(wgt, g)
                    for j in range(TOPK):
                        for c in range(NC):
                            ins = dve.scalar_tensor_tensor(x[s][:, c, :], yg[s][:, c, j, :], w[:, c, j:j + 1],
                                                           x[s][:, c, :], ALU.mult, ALU.add)
                        if j == 0:
                            dve.drain()
                    ins.then_inc(added, 1)

                rounds(dve, step)

            @block.scalar
            def _(act):
                def step(g, s, i):
                    act.wait_ge(added, g + 1)
                    act.dma_start(group(out_g, g), x[s][:]).then_inc(stored[s], 16)

                rounds(act, step)
                for s in range(2):
                    act.wait_ge(stored[s], 16 * (G // 2))


class Constants:

    def __init__(self, m, wr_dram):
        self.wr_dram = wr_dram
        self.ident = m.sb("ident", [P, P])
        self.before = m.sb("before", [P, P], BF16)
        self.ones = m.sb("ones", [P, P], BF16)
        self.causal = m.sb("causal", [P, P])
        self.heads = m.sb("heads", [P, HH])
        self.same_head = m.sb("same_head", [P, P])
        self.expert_i = m.sb("expert_i", [P, E], I32)
        self.region_i = m.sb("region_i", [P, E], I32)
        self.later_i = m.sb("later_i", [P, G // GB, GB], I32)
        self.expert = m.sb("expert", [P, E])
        self.region = m.sb("region", [P, E])
        self.later = m.sb("later", [P, G])
        self.passed = m.sem("passed")
        self.wr = m.sb("wr", [P, KD, E])
        self.wqk = [m.sb(f"wqk{i}", [P, KD, 2 * D], F32R) for i in range(2)]
        self.wvk = [m.sb(f"wvk{i}", [P, KD, 2 * D], F32R) for i in range(2)]
        self.fold = [m.sb(f"fold{i}", [P, KD, D], F32R) for i in range(2)]


def macaron(nc, x, wqT, wkT, wvT, wcT, ltriT, wr, w1, w3, w2, out):
    xe = nc.dram_tensor("expert_rows", (SLOTS, D), F32).ap()
    ye = nc.dram_tensor("expert_out", (SLOTS + CAP, D), F32).ap()
    x2 = nc.dram_tensor("x2", (T, D), F32).ap()
    experts = (w1, w3, w2)
    with ExitStack() as ctx:
        m = Memory(nc, ctx, "c_")
        k = Constants(m, wr)
        slot_a = [m.sb("wa_hi", [P, WCOLS], F32R), m.sb("wa_lo", [P, WCOLS], F32R)]
        routes = [(m.sb(f"wgt{i}", [P, G, NC, TOPK]), m.sb(f"gidx{i}", [P, G, NC, TOPK], I32),
                   m.sb(f"ntile{i}", [P, E], I32), m.sb(f"first{i}", [P, E + 1], I32)) for i in range(2)]
        setup_phase(nc, k, dict(wqT=wqT, wkT=wkT, wvT=wvT, wcT=wcT, ltriT=ltriT, wr=wr))
        route_phase(nc, k, x, xe, ye, [slot_a], experts, routes[0])
        expert_phase(nc, k, "e1_", xe, ye, slot_a, experts, routes[0], clear=True)
        middle_phase(nc, k, x, x2, xe, ye, routes[0], routes[1])
        expert_phase(nc, k, "e2_", xe, ye, slot_a, experts, routes[1], clear=False)
        final_phase(nc, k, x2, ye, out, routes[1])


def kernel(L0_attn_X, L0_attn_Wq, L0_attn_Wk, L0_attn_Wv, L0_attn_Wc, L0_attn_Ltri,
           L0_ffn_Wr, L0_ffn_W1, L0_ffn_W3, L0_ffn_W2):
    import numpy as np
    import concourse.bacc as bacc
    from concourse.bass_utils import run_bass_kernel_spmd

    shape = np.shape(L0_attn_X)
    arrays = {
        "x": np.asarray(L0_attn_X).reshape(T, D),
        "wqT": np.asarray(L0_attn_Wq).T, "wkT": np.asarray(L0_attn_Wk).T,
        "wvT": np.asarray(L0_attn_Wv).T, "wcT": np.asarray(L0_attn_Wc).T,
        "ltriT": np.asarray(L0_attn_Ltri).transpose(0, 2, 1),
        "wr": np.asarray(L0_ffn_Wr), "w1": np.asarray(L0_ffn_W1),
        "w3": np.asarray(L0_ffn_W3), "w2": np.asarray(L0_ffn_W2),
    }
    arrays = {n: np.ascontiguousarray(a) for n, a in arrays.items()}
    nc = bacc.Bacc("TRN2", target_bir_lowering=False, num_devices=1)
    args = [nc.dram_tensor(n, a.shape, mybir.dt.from_np(a.dtype), kind="ExternalInput").ap()
            for n, a in arrays.items()]
    out = nc.dram_tensor("out", (T, D), F32, kind="ExternalOutput").ap()
    macaron(nc, *args, out)
    result = run_bass_kernel_spmd(nc, [arrays], core_ids=[0])
    return result.results[0]["out"].reshape(shape)
```

```python
from contextlib import ExitStack

import concourse.bass as bass
from concourse import mybir

F32 = mybir.dt.float32
F32R = mybir.dt.float32r
BF16 = mybir.dt.bfloat16
I32 = mybir.dt.int32
U32 = mybir.dt.uint32
ALU = mybir.AluOpType
ACT = mybir.ActivationFunctionType
AX_X = mybir.AxisListType.X

P = 128
T = 4 * 2048
D = 256
KD = D // P
E = 8
TOPK = 2
F = 1024
KF = F // P
CAP = -(-T * TOPK * 5 // (4 * E))
H = 16
HD = D // H
HH = P // HD
NC = 4
GT = NC * P
G = T // GT
GB = 2048 // GT
TS = 256
TPE = CAP // TS
SLOTS = E * CAP
FJ = KF // 2
WCOLS = KD * 2 * F + KF * D
W2AT = KD * 2 * F
PIECES = 12
PIECE = WCOLS // PIECES
NR = 8
GR = T // (NR * P)
ROWS = T + TS
SCOLS = SLOTS // P
EPS = 1e-5
CLAMP = 10000.0
DROPPED = 1.0e6
RSQRT_SEED = float(0x5F3759DF)
VSTEP = P + HD


def wait(eng, sem, value):
    if isinstance(value, int) and value <= 0:
        return
    eng.wait_ge(sem, value)


def wait_alone(eng, sem, value, passed):
    eng.wait_ge(sem, value)
    eng.sem_inc(passed, 1)


def mm3(pe, out, a, b, first, last):
    pe.matmul(out, a[0], b[0], start=first, stop=False)
    pe.matmul(out, a[0], b[1], start=False, stop=False)
    return pe.matmul(out, a[1], b[0], start=False, stop=last)


class Memory:

    def __init__(self, nc, ctx, prefix):
        self.nc, self.ctx, self.prefix = nc, ctx, prefix

    def sb(self, name, shape, dt=F32):
        return self.ctx.enter_context(self.nc.sbuf_tensor(self.prefix + name, shape, dt))

    def ps(self, name):
        return self.ctx.enter_context(self.nc.psum_tensor(self.prefix + name, [P, 512], F32))

    def sem(self, name):
        return self.ctx.enter_context(self.nc.semaphore(self.prefix + name))


def inverse_root(dve, y, seed, v):
    dve.tensor_scalar(seed, v.bitcast(I32), 1, None, ALU.logical_shift_right)
    dve.drain()
    dve.tensor_scalar(y.bitcast(I32), seed, -1.0, RSQRT_SEED, ALU.mult, ALU.add)
    dve.drain()
    for _ in range(3):
        s = seed.bitcast(F32)
        dve.tensor_tensor(s, y, y, ALU.mult)
        dve.drain()
        dve.scalar_tensor_tensor(s, s, -0.5, v, ALU.mult, ALU.mult)
        dve.drain()
        dve.scalar_tensor_tensor(y, s, 1.5, y, ALU.add, ALU.mult)
        dve.drain()


class Norm:

    def __init__(self, m, name, n):
        self.n = n
        self.stats = m.sb(name + "_stats", [P, n, 6])
        self.mv = m.sb(name + "_mv", [P, n, 2])
        self.var = m.sb(name + "_var", [P, n])
        self.rstd = m.sb(name + "_rstd", [P, n])
        self.seed = m.sb(name + "_seed", [P, n], I32)

    def run(self, dve, src, dst, done):
        for c in range(self.n):
            dve.bn_stats(self.stats[:, c, :], src(c))
        dve.drain()
        for c in range(self.n):
            dve.bn_aggr(self.mv[:, c, :], self.stats[:, c, :])
        dve.drain()
        dve.tensor_scalar(self.var[:], self.mv[:, :, 1], EPS, None, ALU.add)
        dve.drain()
        inverse_root(dve, self.rstd[:], self.seed[:], self.var[:])
        for c in range(self.n):
            ins = dve.tensor_scalar(dst[:, c, :], src(c), self.mv[:, c, 0:1], self.rstd[:, c:c + 1],
                                    ALU.subtract, ALU.mult)
        ins.then_inc(done, 1)


class Router:
    LG_AT, RANK_AT = 0, 128

    def __init__(self, m, k, n, turn_banks, lg_bank, rank_bank, table, bufs):
        self.k, self.n, self.table = k, n, table
        self.turn_banks, self.lg_bank, self.rank_bank = turn_banks, lg_bank, rank_bank
        self.xnT = m.sb("r_xnT", [P, KD, n * P])
        self.lg = m.sb("r_lg", [P, n, E])
        self.top = m.sb("r_top", [P, n, 8])
        self.topi = m.sb("r_topi", [P, n, 8], U32)
        self.idx = m.sb("r_idx", [P, n, TOPK])
        self.oh = m.sb("r_oh", [P, n, TOPK, E])
        self.chosen = m.sb("r_chosen", [P, n, E], BF16)
        self.diff = m.sb("r_diff", [P, n])
        self.exp = m.sb("r_exp", [P, n])
        self.den = m.sb("r_den", [P, n])
        self.prob = m.sb("r_prob", [P, n, TOPK])
        self.pos = m.sb("r_pos", [P, n, E])
        self.ohpos = m.sb("r_ohpos", [P, n, TOPK, E])
        self.slotf = m.sb("r_slotf", [P, n, TOPK])
        self.slot = m.sb("r_slot", [P, n, TOPK], I32)
        self.row = m.sb("r_row", [P, n, TOPK], I32)
        self.col = m.sb("r_col", [P, n, TOPK], I32)
        self.rank = m.sb("r_rank", [P, n, TOPK])
        self.drop = m.sb("r_drop", [P, n, TOPK])
        self.at = m.sb("r_at", [P, n, TOPK])
        self.entry = [m.sb(f"r_entry{b}", [P, n, TOPK, 2]) for b in range(bufs)]
        self.entry_at = [m.sb(f"r_entry_at{b}", [P, n, TOPK], I32) for b in range(bufs)]
        self.bufs = bufs
        self.more = m.sb("r_more", [P, E])
        self.seen = m.sb("r_seen", [P, E], BF16)
        self.xn_ready = m.sem("r_xn_ready")
        self.turned = m.sem("r_turned")
        self.xnT_ready = m.sem("r_xnT_ready")
        self.lg_made = m.sem("r_lg_made")
        self.diff_ready = m.sem("r_diff_ready")
        self.exp_ready = m.sem("r_exp_ready")
        self.chosen_ready = m.sem("r_chosen_ready")
        self.rank_made = m.sem("r_rank_made")
        self.rank_read = m.sem("r_rank_read")
        self.entry_ready = m.sem("r_entry_ready")
        self.entered = [m.sem(f"r_entered{b}") for b in range(bufs)]
        self.seen_ready = m.sem("r_seen_ready")
        self.count_made = m.sem("r_count_made")

    def start(self, dve):
        dve.memset(self.seen[:], 0.0)
        dve.drain()
        dve.nop().then_inc(self.seen_ready, 1)

    def transposes(self, pe, g, xn):
        pe.wait_ge(self.xn_ready, g + 1)
        for b in range(self.n // 2):
            if b >= len(self.turn_banks):
                pe.wait_ge(self.xnT_ready, self.n // 2 * g + b + 1 - len(self.turn_banks))
            bank = self.turn_banks[b % len(self.turn_banks)]
            for c in range(2):
                for h in range(KD):
                    at = (h * 2 + c) * P
                    ins = pe.transpose(bank[:, at:at + P], xn[:, 2 * b + c, h * P:(h + 1) * P], self.k.ident[:])
            ins.then_inc(self.turned, 1)

    def keep_xnT(self, act, g):
        for b in range(self.n // 2):
            act.wait_ge(self.turned, self.n // 2 * g + b + 1)
            bank = self.turn_banks[b % len(self.turn_banks)]
            act.activation(self.xnT[:, :, b * 2 * P:(b + 1) * 2 * P],
                           bank[:].rearrange("p (h t) -> p h t", h=KD), ACT.Copy).then_inc(self.xnT_ready, 1)

    def logits(self, pe, g):
        pe.wait_ge(self.xnT_ready, self.n // 2 * (g + 1))
        for c in range(self.n):
            at = self.LG_AT + c * E
            for h in range(KD):
                ins = pe.matmul(self.lg_bank[:, at:at + E], self.xnT[:, h, c * P:(c + 1) * P], self.k.wr[:, h, :],
                                start=(h == 0), stop=(h == KD - 1))
        ins.then_inc(self.lg_made, 1)

    def choose(self, dve, g):
        n = self.n
        dve.wait_ge(self.lg_made, g + 1)
        dve.tensor_scalar(self.lg[:], self.lg_bank[:, self.LG_AT:self.LG_AT + n * E].rearrange("p (c e) -> p c e", c=n),
                          -CLAMP, CLAMP, ALU.max, ALU.min)
        dve.drain()
        for c in range(n):
            dve.max(self.top[:, c, :], self.lg[:, c, :])
        dve.drain()
        dve.tensor_tensor(self.diff[:], self.top[:, :, 1], self.top[:, :, 0], ALU.subtract).then_inc(self.diff_ready, 1)
        for c in range(n):
            dve.max_index(self.topi[:, c, :], self.top[:, c, :], self.lg[:, c, :])
        dve.drain()
        dve.tensor_copy(self.idx[:], self.topi[:, :, 0:TOPK])
        dve.drain()
        dve.tensor_tensor(self.oh[:], self.k.expert[:].unsqueeze(1).unsqueeze(1).broadcast_to([P, n, TOPK, E]),
                          self.idx[:].unsqueeze(3).broadcast_to([P, n, TOPK, E]), ALU.is_equal)
        dve.drain()
        dve.tensor_tensor(self.chosen[:], self.oh[:, :, 0, :], self.oh[:, :, 1, :],
                          ALU.add).then_inc(self.chosen_ready, 1)

    def weigh(self, act, g):
        act.wait_ge(self.diff_ready, g + 1)
        act.activation(self.exp[:], self.diff[:], ACT.Exp).then_inc(self.exp_ready, 1)

    def rank_out(self):
        return self.rank_bank[:, self.RANK_AT:self.RANK_AT + self.n * E].rearrange("p (c e) -> p c e", c=self.n)

    def ranks(self, pe, g):
        n, out = self.n, self.rank_out()
        pe.wait_ge(self.chosen_ready, g + 1)
        pe.wait_ge(self.seen_ready, g + 1)
        pe.matmul(out, self.k.before[:], self.chosen[:], start=True, stop=False)
        for c in range(1, n):
            pe.matmul(out[:, c:n, :], self.k.ones[:],
                      self.chosen[:, c - 1:c, :].broadcast_to([P, n - c, E]), start=False, stop=False)
        pe.matmul(out, self.k.ones[:], self.seen[:].unsqueeze(1).broadcast_to([P, n, E]),
                  start=False, stop=True).then_inc(self.rank_made, 1)

    def place(self, dve, g, b, entered):
        n, entry, entry_at = self.n, self.entry[b], self.entry_at[b]
        dve.wait_ge(self.rank_made, g + 1)
        dve.tensor_tensor(self.pos[:], self.rank_out(),
                          self.k.region[:].unsqueeze(1).broadcast_to([P, n, E]), ALU.add).then_inc(self.rank_read, 1)
        dve.tensor_reduce(self.more[:], self.chosen[:].rearrange("p c e -> p e c"), AX_X, ALU.add)
        dve.drain()
        dve.tensor_tensor(self.seen[:], self.seen[:], self.more[:], ALU.add).then_inc(self.seen_ready, 1)
        dve.tensor_tensor(self.ohpos[:], self.oh[:], self.pos[:].unsqueeze(2).broadcast_to([P, n, TOPK, E]), ALU.mult)
        dve.wait_ge(self.exp_ready, g + 1)
        dve.tensor_scalar(self.den[:], self.exp[:], 1.0, 1e-12, ALU.add, ALU.add)
        dve.drain()
        dve.tensor_reduce(self.slotf[:], self.ohpos[:], AX_X, ALU.add)
        dve.reciprocal(self.prob[:, :, 0], self.den[:])
        dve.drain()
        dve.tensor_copy(self.slot[:], self.slotf[:])
        dve.scalar_tensor_tensor(self.rank[:], self.idx[:], -float(CAP), self.slotf[:], ALU.mult, ALU.add)
        dve.tensor_tensor(self.prob[:, :, 1], self.exp[:], self.prob[:, :, 0], ALU.mult)
        dve.drain()
        dve.tensor_scalar(self.row[:], self.slot[:], P - 1, None, ALU.bitwise_and)
        dve.tensor_scalar(self.col[:], self.slot[:], P.bit_length() - 1, None, ALU.logical_shift_right)
        dve.tensor_scalar(self.drop[:], self.rank[:], float(CAP), DROPPED, ALU.is_ge, ALU.mult)
        dve.drain()
        dve.scalar_tensor_tensor(self.at[:], self.row[:], float(SCOLS), self.col[:], ALU.mult, ALU.add)
        wait(dve, self.entered[b], entered)
        token = self.k.token[:].rearrange("p (g c) -> p g c", c=n)
        token = token[:, g] if isinstance(g, int) else token[:, bass.ds(g, 1)].rearrange("p o c -> p (o c)")
        dve.tensor_copy(entry[:, :, :, 0].bitcast(I32), token.unsqueeze(2).broadcast_to([P, n, TOPK]))
        dve.tensor_scalar(entry[:, :, :, 1], self.prob[:], 0.5, None, ALU.mult)
        dve.drain()
        dve.tensor_tensor(entry_at[:], self.at[:], self.drop[:], ALU.add).then_inc(self.entry_ready, 1)

    def enter(self, pool, g, b):
        wait_alone(pool, self.entry_ready, g + 1, self.k.passed)
        for c in range(self.n):
            for j in range(TOPK):
                pool.indirect_dma_start(
                    self.table, bass.IndirectOffsetOnAxis(ap=self.entry_at[b][:, c, j:j + 1], axis=0),
                    self.entry[b][:, c, j, :], None,
                    bounds_check=SLOTS - 1, oob_is_err=False).then_inc(self.entered[b], 16)

    def count(self, pe, groups):
        pe.wait_ge(self.seen_ready, groups + 1)
        pe.wait_ge(self.rank_read, groups)
        pe.matmul(self.rank_bank[:, 0:E], self.k.ones[:], self.seen[:], start=True, stop=True).then_inc(self.count_made, 1)

    def tiles(self, dve, ntile, first_tile):
        cnt, cnti, scan, zero = self.lg[:, 0, :], self.topi[:, 0, :].bitcast(I32), self.lg[:, 1, :], self.lg[:, 2, :]
        dve.wait_ge(self.count_made, 1)
        dve.tensor_scalar(cnt, self.rank_bank[:, 0:E], float(CAP), float(TS - 1), ALU.min, ALU.add)
        dve.memset(zero, 0.0)
        dve.drain()
        dve.tensor_copy(cnti, cnt)
        dve.drain()
        dve.tensor_scalar(cnti, cnti, TS.bit_length() - 1, None, ALU.logical_shift_right)
        dve.drain()
        dve.tensor_scalar(cnt, cnti, 1.0, None, ALU.max)
        dve.drain()
        dve.tensor_copy(ntile[:], cnt)
        dve.tensor_tensor_scan(scan, cnt, zero, 0.0, ALU.add, ALU.add)
        dve.memset(first_tile[:, 0:1], 0.0)
        dve.drain()
        dve.tensor_copy(first_tile[:, 1:E + 1], scan)


class Setup:

    def __init__(self, m, k, inputs, bank_b, bank_m):
        self.k, self.inputs, self.pb, self.pm = k, inputs, bank_b, bank_m
        self.raw_qk = m.sb("su_raw_qk", [P, KD, 2 * D])
        self.raw_vk = m.sb("su_raw_vk", [P, KD, 2 * D])
        self.wc = m.sb("su_wc", [P, KD, D])
        self.lt = m.sb("su_lt", [P, KD, HD])
        self.low = m.sb("su_low", [P, P])
        self.lbd = m.sb("su_lbd", [P, KD, P])
        self.bbd = m.sb("su_bbd", [P, KD, P])
        self.wr_loaded, self.loads = m.sem("su_wr_loaded"), m.sem("su_loads")
        self.masks0, self.masks = m.sem("su_masks0"), m.sem("su_masks")
        self.split, self.tri_ready = m.sem("su_split"), m.sem("su_tri_ready")
        self.bbd_made, self.bbd_ready = m.sem("su_bbd_made"), m.sem("su_bbd_ready")
        self.fold_made = m.sem("su_fold_made")

    def load_router(self, q):
        q.dma_start(self.k.wr[:], self.inputs["wr"].rearrange("(k p) n -> p k n", p=P)).then_inc(self.wr_loaded, 16)

    def load(self, q):
        inputs, loads = self.inputs, self.loads

        def by_k(w):
            return w.rearrange("(k p) n -> p k n", p=P)

        q.dma_start(self.raw_qk[:, :, 0:D], by_k(inputs["wqT"])).then_inc(loads, 16)
        q.dma_start(self.raw_qk[:, :, D:2 * D], by_k(inputs["wkT"])).then_inc(loads, 16)
        q.dma_start(self.raw_vk[:, :, 0:D], by_k(inputs["wvT"])).then_inc(loads, 16)
        q.dma_start(self.raw_vk[:, :, D:2 * D], by_k(inputs["wkT"])).then_inc(loads, 16)
        q.dma_start(self.wc[:], by_k(inputs["wcT"])).then_inc(loads, 16)
        q.dma_start(self.lt[:], inputs["ltriT"].rearrange("(a h) k e -> (h k) a e", a=KD)).then_inc(loads, 16)

    def make_masks(self, pool):
        k, masks0 = self.k, self.masks0
        pool.memset(k.ident[:], 0.0)
        pool.memset(k.before[:], 1.0)
        pool.memset(k.causal[:], 1.0)
        pool.memset(k.heads[:], 1.0)
        pool.iota(k.expert_i[:], pattern=[[1, E]], base=0, channel_multiplier=0)
        pool.iota(k.region_i[:], pattern=[[CAP, E]], base=0, channel_multiplier=0)
        pool.iota(k.later_i[:], pattern=[[0, G // GB], [1, GB]], base=0, channel_multiplier=0)
        pool.iota(k.token[:], pattern=[[P, T // P]], base=0, channel_multiplier=1)
        pool.iota(k.spare[:], pattern=[[P, TS // P]], base=T, channel_multiplier=1)
        pool.memset(k.ones[:], 1.0).then_inc(masks0, 1)
        pool.wait_ge(masks0, 1)
        pool.affine_select(out=k.ident[:], in_=k.ident[:], compare_op=ALU.not_equal, fill=1.0,
                           base=0, pattern=[[-1, P]], channel_multiplier=1)
        pool.affine_select(out=k.before[:], in_=k.before[:], compare_op=ALU.is_ge, fill=0.0,
                           base=-1, pattern=[[1, P]], channel_multiplier=-1)
        pool.affine_select(out=k.causal[:], in_=k.causal[:], compare_op=ALU.is_ge, fill=0.0,
                           base=0, pattern=[[1, P]], channel_multiplier=-1)
        pool.affine_select(out=k.heads[:], in_=k.heads[:], compare_op=ALU.is_ge, fill=0.0,
                           base=0, pattern=[[-HD, HH]], channel_multiplier=1).then_inc(masks0, 1)
        pool.wait_ge(masks0, 2)
        pool.affine_select(out=k.heads[:], in_=k.heads[:], compare_op=ALU.is_ge, fill=0.0,
                           base=HD - 1, pattern=[[HD, HH]], channel_multiplier=-1).then_inc(masks0, 1)
        pool.wait_ge(masks0, 3)
        pool.tensor_copy(k.same_head[:].rearrange("p (h e) -> p h e", e=HD),
                         k.heads[:].unsqueeze(2).broadcast_to([P, HH, HD])).then_inc(self.masks, 1)

    def numbers(self, dve):
        k = self.k
        dve.wait_ge(self.masks0, 1)
        dve.tensor_copy(k.expert[:], k.expert_i[:])
        dve.tensor_copy(k.region[:], k.region_i[:])
        dve.tensor_scalar(k.later[:], k.later_i[:].rearrange("p a b -> p (a b)"), 0.5, None, ALU.is_gt)

    def spread_tri(self, dve):
        k = self.k
        dve.wait_ge(self.masks, 1)
        dve.tensor_tensor(self.low[:], k.causal[:], k.same_head[:], ALU.mult)
        dve.drain()
        dve.wait_ge(self.loads, 16 * 6)
        for a in range(KD):
            dve.tensor_tensor(self.lbd[:, a, :].rearrange("p (h e) -> p h e", e=HD),
                              self.low[:].rearrange("p (h e) -> p h e", e=HD),
                              self.lt[:, a, :].unsqueeze(1).broadcast_to([P, HH, HD]),
                              ALU.mult).then_inc(self.tri_ready, 1)

    def low_parts(self, dve):
        k = self.k
        dve.wait_ge(self.split, 2)
        dve.tensor_tensor(k.wqk[1][:], self.raw_qk[:], k.wqk[0][:].bitcast(F32), ALU.subtract)
        dve.tensor_tensor(k.wvk[1][:], self.raw_vk[:], k.wvk[0][:].bitcast(F32), ALU.subtract)
        dve.wait_ge(self.split, 3)
        dve.tensor_tensor(k.fold[1][:].rearrange("p a n -> p (a n)"), self.pm[:],
                          k.fold[0][:].bitcast(F32).rearrange("p a n -> p (a n)"), ALU.subtract)

    def high_parts(self, act):
        k = self.k
        act.wait_ge(self.loads, 16 * 6)
        act.activation(k.wqk[0][:], self.raw_qk[:], ACT.Copy).then_inc(self.split, 1)
        act.activation(k.wvk[0][:], self.raw_vk[:], ACT.Copy).then_inc(self.split, 1)
        act.wait_ge(self.bbd_made, 1)
        act.activation(self.bbd[:], self.pb[:, 0:KD * P].rearrange("p (a n) -> p a n", a=KD),
                       ACT.Copy).then_inc(self.bbd_ready, 1)
        act.wait_ge(self.fold_made, 1)
        act.activation(k.fold[0][:], self.pm[:].rearrange("p (a n) -> p a n", a=KD), ACT.Copy).then_inc(self.split, 1)

    def fold_heads(self, pe):
        pe.wait_ge(self.tri_ready, KD)
        for a in range(KD):
            ins = pe.matmul(self.pb[:, a * P:(a + 1) * P], self.lbd[:, a, :], self.lbd[:, a, :], start=True, stop=True)
        ins.then_inc(self.bbd_made, 1)
        pe.wait_ge(self.bbd_ready, 1)
        for a in range(KD):
            ins = pe.matmul(self.pm[:, a * D:(a + 1) * D], self.bbd[:, a, :], self.wc[:, a, :], start=True, stop=True)
        ins.then_inc(self.fold_made, 1)


def piece(t, q):
    return t[:, q * PIECE:(q + 1) * PIECE]


def load_expert(sp, w, e, raw, raw_loaded, n):
    w1, w3, w2 = w
    pick = (lambda t: t[e]) if isinstance(e, int) else (lambda t: t[bass.ds(e, 1)].rearrange("o a b -> (o a) b"))
    for q in range(PIECES):
        wait(sp, raw_loaded[q % 2], 16 * (PIECES // 2 * n + q // 2))
        if q * PIECE < W2AT:
            kk, col = divmod(q * PIECE, 2 * F)
            src = pick(w1 if col < F else w3)[kk * P:(kk + 1) * P, col % F:col % F + PIECE]
            dst = piece(raw, q)
        else:
            row = (q * PIECE - W2AT) // D * P
            src = pick(w2)[row:row + PIECE // D * P, :].rearrange("(k p) d -> p k d", p=P)
            dst = piece(raw, q).rearrange("p (k d) -> p k d", d=D)
        sp.dma_start(dst, src).then_inc(raw_loaded[q % 2], 16)


def wait_raw(eng, raw_loaded, n, q=None):
    if q is None:
        for b in range(2):
            eng.wait_ge(raw_loaded[b], 16 * (PIECES // 2) * (n + 1))
    else:
        eng.wait_ge(raw_loaded[q % 2], 16 * (PIECES // 2 * n + q // 2 + 1))


def route_phase(nc, k, attention, x_in, xn_out, x1_out, out, tables, w, slot_a, raw, raw_loaded, tiles_out):
    ntile, first_tile = tiles_out
    with ExitStack() as ctx:
        m = Memory(nc, ctx, "r1_")
        xin = [m.sb(f"xin{s}", [P, NR, D]) for s in range(2)]
        xn = [m.sb(f"xn{s}", [P, NR, D]) for s in range(2)]
        zeros = m.sb("zeros", [P, D])
        unfilled = m.sb("unfilled", [P, SCOLS, 2])
        turn_banks = [m.ps(f"turn{i}") for i in range(4)]
        r = Router(m, k, NR, turn_banks, m.ps("lg"), m.ps("rank"), tables[0], 2)
        norm = Norm(m, "n", NR)
        su = Setup(m, k, attention, m.ps("pb"), m.ps("pm"))
        x_loaded = [m.sem(f"x_loaded{s}") for s in range(2)]
        x_copied = [m.sem(f"x_copied{s}") for s in range(2)]
        xn_stored = [m.sem(f"xn_stored{s}") for s in range(2)]
        w_high = m.sem("w_high")
        w_low = m.sem("w_low")
        blank = m.sem("blank")
        cleared = m.sem("cleared")

        x_g, x1_g, xn_g = (t[0:T, :].rearrange("(g c p) d -> g p c d", p=P, c=NR) for t in (x_in, x1_out, xn_out))

        def group(t, g):
            return t[g] if isinstance(g, int) else t[bass.ds(g, 1)].rearrange("o p c d -> p (o c) d")

        def rounds(eng, step):
            for s in range(2):
                step(s, s, 0)
            with eng.Fori(1, GR // 2) as i:
                for s in range(2):
                    step(2 * i + s, s, i)

        with nc.Block() as block:
            @block.sync
            def _(sp):
                def load(g, s):
                    sp.dma_start(xin[s][:], group(x_g, g)).then_inc(x_loaded[s], 16)

                def next_load(i, s):
                    sp.wait_ge(r.xn_ready, 2 * i + s + 1)
                    sp.wait_ge(x_copied[s], 16 * i + 16)
                    load(2 * i + s + 2, s)

                load(0, 0)
                su.load_router(sp)
                load(1, 1)
                su.load(sp)
                for s in range(2):
                    next_load(0, s)
                load_expert(sp, w, 0, raw, raw_loaded, 0)
                with sp.Fori(1, GR // 2 - 1) as i:
                    for s in range(2):
                        next_load(i, s)
                sp.wait_ge(w_low, 1)
                load_expert(sp, w, 1, raw, raw_loaded, 1)
                wait_raw(sp, raw_loaded, 1)

            @block.scalar
            def _(act):
                act.wait_ge(blank, 1)
                for i in range(2):
                    act.dma_start(tables[i].rearrange("(p n) c -> p (n c)", p=P),
                                  unfilled[:].rearrange("p n c -> p (n c)")).then_inc(cleared, 16)
                for t in (xn_out, x1_out, out):
                    act.dma_start(t[T:ROWS, :].rearrange("(r p) d -> p r d", p=P),
                                  zeros[:].unsqueeze(1).broadcast_to([P, TS // P, D])).then_inc(cleared, 16)

                def step(g, s, i):
                    act.wait_ge(x_loaded[s], 16 * i + 16)
                    act.dma_start(group(x1_g, g), xin[s][:]).then_inc(x_copied[s], 16)
                    r.keep_xnT(act, g)
                    act.dma_start(group(xn_g, g), xn[s][:]).then_inc(xn_stored[s], 16)
                    r.weigh(act, g)
                    if isinstance(g, int) and g == 0:
                        su.high_parts(act)

                rounds(act, step)
                wait_raw(act, raw_loaded, 0)
                act.activation(slot_a[0][:], raw[:], ACT.Copy).then_inc(w_high, 1)
                act.wait_ge(cleared, 16 * 5)
                for s in range(2):
                    act.wait_ge(x_copied[s], 16 * (GR // 2))
                    act.wait_ge(xn_stored[s], 16 * (GR // 2))

            @block.vector
            def _(dve):
                def ln(g, s, i):
                    dve.wait_ge(x_loaded[s], 16 * (i + 1))
                    wait(dve, xn_stored[s], 16 * i)
                    norm.run(dve, lambda c: xin[s][:, c, :], xn[s], r.xn_ready)

                def step(g, s, i, last=False):
                    r.choose(dve, g)
                    r.place(dve, g, s, 16 * NR * TOPK * i)
                    if not last:
                        ln(g + 2, s, i + 1)
                    if isinstance(g, int) and g == 0:
                        su.low_parts(dve)

                su.numbers(dve)
                dve.memset(zeros[:], 0.0)
                dve.memset(unfilled[:], 0.0)
                dve.drain()
                dve.tensor_copy(unfilled[:].rearrange("p (n s) c -> p n s c", s=TS // P)[:, :, :, 0].bitcast(I32),
                                k.spare[:].unsqueeze(1).broadcast_to([P, SCOLS * P // TS, TS // P])).then_inc(blank, 1)
                r.start(dve)
                ln(0, 0, 0)
                ln(1, 1, 0)
                su.spread_tri(dve)
                step(0, 0, 0)
                step(1, 1, 0)
                with dve.Fori(1, GR // 2 - 1) as i:
                    for s in range(2):
                        step(2 * i + s, s, i)
                step(GR - 2, 0, GR // 2 - 1, last=True)
                step(GR - 1, 1, GR // 2 - 1, last=True)
                dve.wait_ge(w_high, 1)
                dve.tensor_tensor(slot_a[1][:], raw[:], slot_a[0][:].bitcast(F32), ALU.subtract).then_inc(w_low, 1)
                r.tiles(dve, ntile, first_tile)

            @block.gpsimd
            def _(pool):
                su.make_masks(pool)
                pool.wait_ge(cleared, 16 * 5)
                rounds(pool, lambda g, s, i: r.enter(pool, g, s))
                for s in range(2):
                    pool.wait_ge(r.entered[s], 16 * NR * TOPK * (GR // 2))

            @block.tensor
            def _(pe):
                def step(g, s, i):
                    r.transposes(pe, g, xn[s])
                    wait(pe, r.chosen_ready, g)
                    r.logits(pe, g)
                    wait(pe, r.rank_read, g)
                    r.ranks(pe, g)

                pe.wait_ge(su.masks, 1)
                pe.wait_ge(su.wr_loaded, 16)
                step(0, 0, 0)
                su.fold_heads(pe)
                step(1, 1, 0)
                with pe.Fori(1, GR // 2) as i:
                    for s in range(2):
                        step(2 * i + s, s, i)
                r.count(pe, GR)


def expert_phase(nc, k, name, xn, acc, table, w, slot_a, raw, raw_loaded, tiles, loaded):
    ntile, first_tile = tiles
    with ExitStack() as ctx:
        m = Memory(nc, ctx, name)
        slot_b = [m.sb("wb_hi", [P, WCOLS], F32R), m.sb("wb_lo", [P, WCOLS], F32R)]
        slots = [slot_a, slot_b]
        entries = m.sb("entries", [P, E * TPE, TS // P, 2])
        token = m.sb("token", [P, 2], I32)
        held_token = m.sb("held_token", [P, 2], I32)
        held_weight = m.sb("held_weight", [P, 2])
        y_token = m.sb("y_token", [P, 2], I32)
        y_weight = m.sb("y_weight", [P, 2])
        xrow = m.sb("xrow", [P, 2, D])
        xT = [m.sb("xT_hi", [P, KD, TS], F32R), m.sb("xT_lo", [P, KD, TS], F32R)]
        gate = m.sb("gate", [P, 2, 512])
        hid = m.sb("hid", [P, 2, 512])
        h = [m.sb("h_hi", [P, KF * TS], F32R), m.sb("h_lo", [P, KF * TS], F32R)]
        yrow = m.sb("yrow", [P, 2, D])
        ps1 = [m.ps(f"ps1_{b}") for b in range(2)]
        ps3 = [m.ps(f"ps3_{b}") for b in range(2)]
        psx = m.ps("psx")
        psy = m.ctx.enter_context(nc.psum_tensor(name + "psy", [P, 2, 512], F32))

        entries_loaded = m.sem("entries_loaded")
        token_ready = m.sem("token_ready")
        held = m.sem("held")
        y_meta = m.sem("y_meta")
        x_loaded = m.sem("x_loaded")
        x_turned = m.sem("x_turned")
        x_high = m.sem("x_high")
        x_ready = m.sem("x_ready")
        h_made = m.sem("h_made")
        gated = m.sem("gated")
        hid_ready = m.sem("hid_ready")
        h_high = m.sem("h_high")
        h_ready = m.sem("h_ready")
        y_made = m.sem("y_made")
        y_kept = m.sem("y_kept")
        y_added = m.sem("y_added")
        w_high = m.sem("w_high")
        w_low = m.sem("w_low")

        def experts(eng, tile_body):
            with eng.Fori(0, E // 2) as i:
                for s in range(2):
                    e = i * 2 + s
                    f = eng.value_load(first_tile[0:1, bass.ds(e, 1)], min_val=0, max_val=E * TPE)
                    n = eng.value_load(ntile[0:1, bass.ds(e, 1)], min_val=1, max_val=TPE)
                    tile_body(e, s, 0, f)
                    with eng.Fori(1, n) as t:
                        tile_body(e, s, t, eng.snap(f + t))

        def total(eng):
            return eng.value_load(first_tile[0:1, E:E + 1], min_val=E, max_val=E * TPE)

        def first_of(t):
            return isinstance(t, int)

        with nc.Block() as block:
            @block.sync
            def _(sp):
                sp.dma_start(entries[:].rearrange("p n s c -> p (n s c)"),
                             table.rearrange("(p n) c -> p (n c)", p=P)).then_inc(entries_loaded, 16)
                if loaded > 2:
                    load_expert(sp, w, 1, raw, raw_loaded, loaded - 1)
                with sp.Fori(0, E - 2) as e:
                    sp.wait_ge(w_low, PIECES * (e + 2))
                    load_expert(sp, w, e + 2, raw, raw_loaded, e + loaded)
                sp.wait_ge(w_low, PIECES * E)
                load_expert(sp, w, 0, raw, raw_loaded, loaded + E - 2)
                wait_raw(sp, raw_loaded, loaded + E - 2)

            @block.gpsimd
            def _(pool):
                def gather():
                    for sub in range(2):
                        pool.indirect_dma_start(
                            xrow[:, sub, :], None, xn,
                            bass.IndirectOffsetOnAxis(ap=token[:, sub:sub + 1], axis=0),
                            bounds_check=ROWS - 1, oob_is_err=True).then_inc(x_loaded, 16)

                def add():
                    for sub in range(2):
                        pool.indirect_dma_start(
                            acc, bass.IndirectOffsetOnAxis(ap=y_token[:, sub:sub + 1], axis=0),
                            yrow[:, sub, :], None, bounds_check=ROWS - 1, oob_is_err=True,
                            compute_op=ALU.add).then_inc(y_added, 16)

                def hold(at):
                    pool.tensor_copy(held_weight[:], entries[:, at, :, 1].rearrange("p o s -> p (o s)"))
                    pool.tensor_copy(held_token[:], entries[:, at, :, 0].rearrange("p o s -> p (o s)").bitcast(I32)
                                     ).then_inc(held, 1)

                def add_last(g):
                    pool.wait_ge(y_added, 32 * g + 32)
                    wait_alone(pool, held, g + 1, k.passed)
                    pool.tensor_copy(y_weight[:], held_weight[:])
                    pool.tensor_copy(y_token[:], held_token[:]).then_inc(y_meta, 1)

                def tile(e, s, t, g):
                    at = bass.ds(e * TPE + t, 1)
                    wait_alone(pool, x_turned, g + 1, k.passed)
                    pool.tensor_copy(token[:], entries[:, at, :, 0].rearrange("p o s -> p (o s)").bitcast(I32)
                                     ).then_inc(token_ready, 1)
                    wait_alone(pool, token_ready, g + 1, k.passed)
                    gather()
                    add_last(g)
                    wait_alone(pool, y_meta, g + 1, k.passed)
                    hold(at)
                    wait_alone(pool, y_kept, g + 1, k.passed)
                    add()

                pool.memset(yrow[:], 0.0)
                pool.memset(held_weight[:], 0.0)
                pool.tensor_copy(held_token[:], k.spare[:])
                pool.tensor_copy(y_token[:], k.spare[:]).then_inc(held, 1)
                pool.nop().then_inc(y_kept, 1)
                wait_alone(pool, held, 1, k.passed)
                add()
                pool.wait_ge(entries_loaded, 16)
                experts(pool, tile)
                n = total(pool)
                wait_alone(pool, x_turned, n + 1, k.passed)
                gather()
                add_last(n)
                wait_alone(pool, y_meta, n + 1, k.passed)
                wait_alone(pool, y_kept, n + 1, k.passed)
                add()
                wait_alone(pool, y_added, 32 * n + 64, k.passed)
                wait_alone(pool, x_loaded, 32 * n + 32, k.passed)

            @block.tensor
            def _(pe):
                pe.nop().then_inc(x_turned, 1)
                pe.nop().then_inc(y_made, 1)

                def turn(n_loaded):
                    pe.wait_ge(x_loaded, n_loaded)
                    for half in range(KD):
                        for sub in range(2):
                            at = half * TS + sub * P
                            ins = pe.transpose(psx[:, at:at + P], xrow[:, sub, half * P:(half + 1) * P], k.ident[:])
                    ins.then_inc(x_turned, 1)

                def tile(e, s, t, g):
                    hi, lo = slots[s]

                    def wt(at):
                        return hi[:, at:at + P], lo[:, at:at + P]

                    def w2t(f):
                        at = W2AT + f * D
                        return hi[:, at:at + D], lo[:, at:at + D]

                    if first_of(t):
                        pe.wait_ge(w_low, PIECES * (e + 1))
                    pe.wait_ge(x_ready, g + 1)
                    for j in range(FJ):
                        pe.wait_ge(hid_ready, 4 * g + j + 1)
                        for fi in range(2):
                            f = 2 * j + fi
                            for ps, base in ((ps1[j % 2], 0), (ps3[j % 2], F)):
                                for kk in range(KD):
                                    ins = mm3(pe, ps[:, fi * TS:(fi + 1) * TS], wt(kk * 2 * F + base + f * P),
                                              (xT[0][:, kk, :], xT[1][:, kk, :]), kk == 0, kk == KD - 1)
                        ins.then_inc(h_made, 1)
                    turn(32 * g + 64)
                    pe.wait_ge(y_kept, g + 1)
                    for j in range(FJ):
                        pe.wait_ge(h_ready, 4 * g + j + 1)
                        for fi in range(2):
                            f = 2 * j + fi
                            for sub in range(2):
                                at = f * TS + sub * P
                                ins = mm3(pe, psy[:, sub, 0:D], (h[0][:, at:at + P], h[1][:, at:at + P]), w2t(f),
                                          f == 0, f == KF - 1)
                    ins.then_inc(y_made, 1)

                turn(32)
                experts(pe, tile)

            with_pair = (range(0, 2), range(2, 4), range(4, 6), range(6, 7))
            before_y, behind_y = range(7, 10), range(10, PIECES)

            @block.scalar
            def _(act):
                def high_w(e, s, q):
                    wait_raw(act, raw_loaded, e + loaded - 1, q)
                    act.activation(piece(slots[1 - s][0], q), piece(raw, q), ACT.Copy).then_inc(w_high, 1)

                def high_x(n):
                    act.wait_ge(x_turned, n)
                    act.activation(xT[0][:], psx[:].rearrange("p (k t) -> p k t", k=KD), ACT.Copy).then_inc(x_high, 1)

                def tile(e, s, t, g):
                    if first_of(t):
                        act.wait_ge(y_made, g + 1)
                    for j in range(FJ):
                        act.wait_ge(h_made, 4 * g + j + 1)
                        act.wait_ge(hid_ready, 4 * g + j + 1)
                        act.activation(gate[:, j % 2, :], ps1[j % 2][:], ACT.Silu).then_inc(gated, 1)
                        act.wait_ge(hid_ready, 4 * g + j + 3)
                        act.activation(h[0][:, j * 512:(j + 1) * 512], hid[:, j % 2, :], ACT.Copy).then_inc(h_high, 1)
                        if first_of(t):
                            for q in with_pair[j]:
                                high_w(e, s, q)
                    high_x(g + 3)
                    if first_of(t):
                        for q in before_y:
                            high_w(e, s, q)
                    act.wait_ge(y_made, g + 2)
                    act.wait_ge(y_meta, g + 2)
                    for sub in range(2):
                        ins = act.activation(yrow[:, sub, :], psy[:, sub, 0:D], ACT.Copy, scale=y_weight[:, sub:sub + 1])
                    ins.then_inc(y_kept, 1)
                    if first_of(t):
                        for q in behind_y:
                            high_w(e, s, q)

                high_x(2)
                experts(act, tile)

            @block.vector
            def _(dve):
                dve.nop().then_inc(hid_ready, 2)
                dve.nop().then_inc(w_low, PIECES)

                def low_w(e, s, q):
                    dve.wait_ge(w_high, PIECES * e + q + 1)
                    dve.tensor_tensor(piece(slots[1 - s][1], q), piece(raw, q), piece(slots[1 - s][0], q).bitcast(F32),
                                      ALU.subtract).then_inc(w_low, 1)

                def low_x(n):
                    dve.wait_ge(x_high, n)
                    dve.tensor_tensor(xT[1][:], psx[:].rearrange("p (k t) -> p k t", k=KD), xT[0][:].bitcast(F32),
                                      ALU.subtract).then_inc(x_ready, 1)

                def tile(e, s, t, g):
                    for j in range(FJ):
                        dve.wait_ge(gated, 4 * g + j + 1)
                        dve.tensor_tensor(hid[:, j % 2, :], ps3[j % 2][:], gate[:, j % 2, :],
                                          ALU.mult).then_inc(hid_ready, 1)
                        dve.wait_ge(h_high, 4 * g + j + 1)
                        at = slice(j * 512, (j + 1) * 512)
                        dve.tensor_tensor(h[1][:, at], hid[:, j % 2, :], h[0][:, at].bitcast(F32),
                                          ALU.subtract).then_inc(h_ready, 1)
                        if first_of(t):
                            for q in with_pair[j]:
                                low_w(e, s, q)
                    low_x(g + 2)
                    if first_of(t):
                        for q in range(before_y[0], PIECES):
                            low_w(e, s, q)

                low_x(1)
                experts(dve, tile)


def middle_phase(nc, k, x1_in, xn_out, x2_out, table, tiles_out):
    ntile, first_tile = tiles_out
    with ExitStack() as ctx:
        m = Memory(nc, ctx, "mi_")
        x1 = m.sb("x1", [P, 2, NC, D])
        xn = m.sb("xn", [P, NC, D])
        xT = [m.sb("xT_hi", [P, KD, GT], F32R), m.sb("xT_lo", [P, KD, GT], F32R)]
        qT = m.sb("qT", [P, KD, GT])
        kT = m.sb("kT", [P, KD, GT])
        qx = [m.sb(f"qx{b}", [P, KD, HH, P]) for b in range(2)]
        vpad = [m.sb(f"vpad{b}", [P, KD * HH * P + P]) for b in range(2)]
        kt = [m.sb(f"kt{b}", [P, D]) for b in range(2)]
        prob = [m.sb(f"prob{b}", [P, H, P]) for b in range(2)]
        state = [m.sb(f"state{b}", [P, KD, P]) for b in range(2)]
        update = m.sb("update", [P, KD, P])
        yT = [m.sb("yT_hi", [P, KD, P], F32R), m.sb("yT_lo", [P, KD, P], F32R)]
        x2 = m.sb("x2", [P, NC, D])
        xn2 = m.sb("xn2", [P, NC, D])
        sc = [m.ps("sc0"), m.ps("sc1")]
        wide = [m.ps("wide0"), m.ps("wide1")]
        vk, yt, kv, op = m.ps("vk"), m.ps("yt"), m.ps("kv"), m.ps("op")
        norm1, norm2 = Norm(m, "n1", NC), Norm(m, "n2", NC)
        r = Router(m, k, NC, wide, wide[1], wide[1], table, 1)

        x_loaded = m.sem("x_loaded")
        xn_ready = m.sem("xn_ready")
        turned = m.sem("turned")
        x_high = m.sem("x_high")
        xT_ready = m.sem("xT_ready")
        qk_made = m.sem("qk_made")
        qk_kept = m.sem("qk_kept")
        qx_ready = m.sem("qx_ready")
        vk_made = m.sem("vk_made")
        vk_kept = m.sem("vk_kept")
        sc_made = m.sem("sc_made")
        prob_ready = m.sem("prob_ready")
        kv_made = m.sem("kv_made")
        state_ready = m.sem("state_ready")
        fresh = m.sem("fresh")
        y_made = m.sem("y_made")
        y_high = m.sem("y_high")
        y_ready = m.sem("y_ready")
        o_made = m.sem("o_made")
        x2_ready = m.sem("x2_ready")
        x2_stored = m.sem("x2_stored")
        xn2_stored = m.sem("xn2_stored")
        vzero = m.sem("vzero")

        x1_g, x2_g, xn_g = (t[0:T, :].rearrange("(g c p) d -> g p c d", p=P, c=NC) for t in (x1_in, x2_out, xn_out))

        def group(t, g):
            return t[g] if isinstance(g, int) else t[bass.ds(g, 1)].rearrange("o p c d -> p (o c) d")

        def slot(g):
            return g % 2

        def x1_of(g, c):
            s = slot(g)
            return x1[:, s, c, :] if isinstance(s, int) else x1[:, bass.ds(s, 1), c, :].rearrange("p o d -> p (o d)")

        def rounds(eng, step):
            step(0, True, False)
            step(1, False, False)
            with eng.Fori(2, G - 1) as g:
                step(g, False, False)
            step(G - 1, False, True)

        with nc.Block() as block:
            @block.sync
            def _(sp):
                def load(g):
                    s = slot(g)
                    dst = x1[:, s] if isinstance(s, int) else x1[:, bass.ds(s, 1)].rearrange("p o c d -> p (o c) d")
                    sp.dma_start(dst, group(x1_g, g)).then_inc(x_loaded, 16)

                def store_xn2(g):
                    wait_alone(sp, r.xn_ready, g + 1, k.passed)
                    sp.dma_start(group(xn_g, g), xn2[:]).then_inc(xn2_stored, 16)

                def step(g, first, last):
                    if not last:
                        wait_alone(sp, xn_ready, g + 1, k.passed)
                        wait(sp, x2_ready, NC * g)
                        load(g + 1)
                    if not first:
                        store_xn2(g - 1)
                    sp.wait_ge(x2_ready, NC * g + NC)
                    sp.dma_start(group(x2_g, g), x2[:]).then_inc(x2_stored, 16)

                load(0)
                rounds(sp, step)
                store_xn2(G - 1)
                sp.wait_ge(x2_stored, 16 * G)
                sp.wait_ge(xn2_stored, 16 * G)

            @block.gpsimd
            def _(pool):
                def set_out(g, c):
                    wait(pool, sc_made, 16 * g + 4 * c - 4)
                    for half in range(KD):
                        pool.wait_ge(qk_kept, 2 * KD * g + half + 1)
                        pool.tensor_tensor(qx[c % 2][:, half],
                                           qT[:, half, c * P:(c + 1) * P].unsqueeze(1).broadcast_to([P, HH, P]),
                                           k.heads[:].unsqueeze(2).broadcast_to([P, HH, P]),
                                           ALU.mult).then_inc(qx_ready, 1)

                def step(g, first, last):
                    for c in range(NC):
                        set_out(g, c)
                    if not first:
                        r.enter(pool, g - 1, 0)

                pool.memset(vpad[0][:], 0.0).then_inc(vzero, 1)
                pool.memset(vpad[1][:], 0.0).then_inc(vzero, 1)
                rounds(pool, step)
                r.enter(pool, G - 1, 0)
                pool.wait_ge(r.entered[0], 16 * NC * TOPK * G)

            @block.tensor
            def _(pe):
                def turn(g):
                    pe.wait_ge(xn_ready, g + 1)
                    for b in range(2):
                        for c in range(2):
                            for h in range(KD):
                                at = (h * 2 + c) * P
                                ins = pe.transpose(wide[b][:, at:at + P], xn[:, 2 * b + c, h * P:(h + 1) * P], k.ident[:])
                        ins.then_inc(turned, 1)

                def project_qk(g):
                    pe.wait_ge(xT_ready, 2 * g + 2)
                    for n in range(2 * KD):
                        if n >= 2:
                            pe.wait_ge(qk_kept, 2 * KD * g + n - 1)
                        for kk in range(KD):
                            cols = slice(n * P, (n + 1) * P)
                            ins = mm3(pe, wide[n % 2][:], (k.wqk[0][:, kk, cols], k.wqk[1][:, kk, cols]),
                                      (xT[0][:, kk, :], xT[1][:, kk, :]), kk == 0, kk == KD - 1)
                        ins.then_inc(qk_made, 1)

                def project_vk(g, c):
                    wait(pe, vk_kept, 2 * (NC * g + c))
                    rows = slice(c * P, (c + 1) * P)
                    for kk in range(KD):
                        ins = mm3(pe, vk[:], (xT[0][:, kk, rows], xT[1][:, kk, rows]),
                                  (k.wvk[0][:, kk, :], k.wvk[1][:, kk, :]), kk == 0, kk == KD - 1)
                    ins.then_inc(vk_made, 1)

                def scores(g, c):
                    for q in range(4):
                        half, u = q // 2, 16 * g + 4 * c + q
                        if c == 0:
                            pe.wait_ge(qk_kept, 2 * KD * g + KD + half + 1)
                        if q % 2 == 0:
                            pe.wait_ge(qx_ready, KD * (NC * g + c) + half + 1)
                        wait(pe, prob_ready, u - 1)
                        pe.matmul(sc[q % 2][:], kT[:, half, c * P:(c + 1) * P],
                                  qx[c % 2][:, half, (q % 2) * 4:(q % 2) * 4 + 4, :],
                                  start=True, stop=True).then_inc(sc_made, 1)

                def vdiag(c, half):
                    at = half * HH * P
                    return vpad[c % 2][:, at:at + HH * VSTEP].rearrange("p (h x) -> p h x", x=VSTEP)[:, :, 0:HD]

                def update_state(g, c):
                    pe.wait_ge(vk_kept, 2 * (NC * g + c + 1))
                    wait(pe, state_ready, NC * g + c)
                    for half in range(KD):
                        ins = pe.matmul(kv[:, half * P:(half + 1) * P], kt[c % 2][:, half * P:(half + 1) * P],
                                        vdiag(c, half), start=True, stop=True)
                    ins.then_inc(kv_made, 1)

                def attend(g, c):
                    wait(pe, state_ready, NC * g + c)
                    if c == 0:
                        pe.wait_ge(fresh, g + 1)
                    wait(pe, y_ready, NC * g + c)
                    for half in range(KD):
                        out = yt[:, half * P:(half + 1) * P]
                        pe.matmul(out, state[c % 2][:, half, :], qT[:, half, c * P:(c + 1) * P], start=True, stop=False)
                        for hh in range(HH):
                            h = half * HH + hh
                            if hh % 4 == 0:
                                pe.wait_ge(prob_ready, 16 * g + 4 * c + h // 4 + 1)
                            ins = pe.matmul(out, vpad[c % 2][:, h * P:(h + 1) * P], prob[c % 2][:, h, :],
                                            start=False, stop=(hh == HH - 1))
                        ins.then_inc(y_made, 1)

                def project_out(g, c):
                    pe.wait_ge(y_ready, NC * g + c + 1)
                    wait(pe, x2_ready, NC * g + c)
                    for half in range(KD):
                        ins = mm3(pe, op[:, 0:D], (yT[0][:, half, :], yT[1][:, half, :]),
                                  (k.fold[0][:, half, :], k.fold[1][:, half, :]), half == 0, half == KD - 1)
                    ins.then_inc(o_made, 1)

                def step(g, first, last):
                    turn(g)
                    project_qk(g)
                    project_vk(g, 0)
                    scores(g, 0)
                    for c in range(NC):
                        update_state(g, c)
                        if c == 3 and not first:
                            r.ranks(pe, g - 1)
                        attend(g, c)
                        if c < NC - 1:
                            project_vk(g, c + 1)
                            scores(g, c + 1)
                        project_out(g, c)
                        if not first and c == 0:
                            pe.wait_ge(qk_kept, 2 * KD * g + 2 * KD)
                            r.transposes(pe, g - 1, xn2)
                        if not first and c == 1:
                            r.logits(pe, g - 1)
                    if not first:
                        pe.wait_ge(r.rank_read, g)

                rounds(pe, step)
                r.transposes(pe, G - 1, xn2)
                r.logits(pe, G - 1)
                r.ranks(pe, G - 1)
                r.count(pe, G)

            @block.scalar
            def _(act):
                def keep_vk(g, c):
                    act.wait_ge(vk_made, NC * g + c + 1)
                    wait(act, y_made, KD * (NC * g + c - 1))
                    dst = vpad[c % 2]
                    for half in range(KD):
                        at = half * HH * P
                        ins = act.activation(
                            dst[:, at:at + HH * VSTEP].rearrange("p (h x) -> p h x", x=VSTEP)[:, :, 0:HD],
                            vk[:, half * P:(half + 1) * P].rearrange("p (h e) -> p h e", e=HD), ACT.Copy)
                    ins.then_inc(vk_kept, 1)
                    act.activation(kt[c % 2][:], vk[:, D:2 * D], ACT.Copy).then_inc(vk_kept, 1)

                def step(g, first, last):
                    for b in range(2):
                        act.wait_ge(turned, 2 * g + b + 1)
                        act.activation(xT[0][:, :, b * 2 * P:(b + 1) * 2 * P],
                                       wide[b][:].rearrange("p (h t) -> p h t", h=KD), ACT.Copy).then_inc(x_high, 1)
                    for n in range(2 * KD):
                        act.wait_ge(qk_made, 2 * KD * g + n + 1)
                        dst = (qT, kT)[n // KD]
                        act.activation(dst[:, n % KD, :], wide[n % 2][:], ACT.Copy).then_inc(qk_kept, 1)
                    keep_vk(g, 0)
                    for c in range(NC):
                        act.wait_ge(y_made, KD * (NC * g + c + 1))
                        wait(act, o_made, NC * g + c)
                        act.activation(yT[0][:], yt[:, 0:KD * P].rearrange("p (a t) -> p a t", a=KD),
                                       ACT.Copy).then_inc(y_high, 1)
                        if c < NC - 1:
                            keep_vk(g, c + 1)
                        if not first and c == 0:
                            r.keep_xnT(act, g - 1)
                        if not first and c == 2:
                            r.weigh(act, g - 1)

                act.wait_ge(vzero, 2)
                rounds(act, step)
                r.keep_xnT(act, G - 1)
                r.weigh(act, G - 1)

            @block.vector
            def _(dve):
                def mask(g, c):
                    wait(dve, y_made, KD * (NC * g + c - 1))
                    for q in range(4):
                        dve.wait_ge(sc_made, 16 * g + 4 * c + q + 1)
                        dve.tensor_tensor(prob[c % 2][:, 4 * q:4 * q + 4, :],
                                          sc[q % 2][:].rearrange("p (h t) -> p h t", h=4),
                                          k.causal[:].unsqueeze(1).broadcast_to([P, 4, P]), ALU.mult).then_inc(prob_ready, 1)

                def advance(g, c):
                    dve.wait_ge(kv_made, NC * g + c + 1)
                    dve.tensor_tensor(update[:], kv[:, 0:KD * P].rearrange("p (a t) -> p a t", a=KD),
                                      k.same_head[:].unsqueeze(1).broadcast_to([P, KD, P]), ALU.mult)
                    dve.drain()
                    wait(dve, y_made, KD * (NC * g + c))
                    dve.tensor_tensor(state[(c + 1) % 2][:], state[c % 2][:], update[:], ALU.add).then_inc(state_ready, 1)

                def low_y(g, c):
                    dve.wait_ge(y_high, NC * g + c + 1)
                    dve.tensor_tensor(yT[1][:], yt[:, 0:KD * P].rearrange("p (a t) -> p a t", a=KD),
                                      yT[0][:].bitcast(F32), ALU.subtract).then_inc(y_ready, 1)

                def add_out(g, c):
                    dve.wait_ge(o_made, NC * g + c + 1)
                    if c == 0:
                        wait(dve, x2_stored, 16 * g)
                    dve.tensor_tensor(x2[:, c, :], op[:, 0:D], x1_of(g, c), ALU.add).then_inc(x2_ready, 1)

                def place(g):
                    r.place(dve, g, 0, 16 * NC * TOPK * g)

                def normed1(g):
                    dve.wait_ge(x_loaded, 16 * g + 16)
                    norm1.run(dve, lambda cc: x1_of(g, cc), xn, xn_ready)

                def step(g, first, last):
                    for b in range(2):
                        dve.wait_ge(x_high, 2 * g + b + 1)
                        cols = slice(b * 2 * P, (b + 1) * 2 * P)
                        dve.tensor_tensor(xT[1][:, :, cols], wide[b][:].rearrange("p (h t) -> p h t", h=KD),
                                          xT[0][:, :, cols].bitcast(F32), ALU.subtract).then_inc(xT_ready, 1)
                    at = slice(g, g + 1) if isinstance(g, int) else bass.ds(g, 1)
                    dve.tensor_scalar(state[0][:], state[0][:], k.later[:, at], None, ALU.mult).then_inc(fresh, 1)
                    mask(g, 0)
                    if not first:
                        normed2(g)
                    for c in range(NC):
                        advance(g, c)
                        if c == 3 and not first:
                            place(g - 1)
                        low_y(g, c)
                        if c < NC - 1:
                            mask(g, c + 1)
                        add_out(g, c)
                        if c == 1 and not last:
                            normed1(g + 1)
                        if c == 2 and not first:
                            r.choose(dve, g - 1)

                def normed2(g):
                    dve.wait_ge(x2_ready, NC * g)
                    wait(dve, xn2_stored, 16 * (g - 1))
                    norm2.run(dve, lambda c: x2[:, c, :], xn2, r.xn_ready)

                dve.memset(state[0][:], 0.0)
                r.start(dve)
                normed1(0)
                rounds(dve, step)
                normed2(G)
                r.choose(dve, G - 1)
                place(G - 1)
                r.tiles(dve, ntile, first_tile)


class Constants:

    def __init__(self, m, wr_dram):
        self.wr_dram = wr_dram
        self.ident = m.sb("ident", [P, P])
        self.before = m.sb("before", [P, P], BF16)
        self.ones = m.sb("ones", [P, P], BF16)
        self.causal = m.sb("causal", [P, P])
        self.heads = m.sb("heads", [P, HH])
        self.same_head = m.sb("same_head", [P, P])
        self.expert_i = m.sb("expert_i", [P, E], I32)
        self.region_i = m.sb("region_i", [P, E], I32)
        self.later_i = m.sb("later_i", [P, G // GB, GB], I32)
        self.token = m.sb("token", [P, T // P], I32)
        self.spare = m.sb("spare", [P, TS // P], I32)
        self.expert = m.sb("expert", [P, E])
        self.region = m.sb("region", [P, E])
        self.later = m.sb("later", [P, G])
        self.passed = m.sem("passed")
        self.wr = m.sb("wr", [P, KD, E])
        self.wqk = [m.sb(f"wqk{i}", [P, KD, 2 * D], F32R) for i in range(2)]
        self.wvk = [m.sb(f"wvk{i}", [P, KD, 2 * D], F32R) for i in range(2)]
        self.fold = [m.sb(f"fold{i}", [P, KD, D], F32R) for i in range(2)]


def macaron(nc, x, wqT, wkT, wvT, wcT, ltriT, wr, w1, w3, w2, out):
    xn = nc.dram_tensor("normed_rows", (ROWS, D), F32).ap()
    x1 = nc.dram_tensor("x1", (ROWS, D), F32).ap()
    tables = [nc.dram_tensor(f"table{i}", (SLOTS, 2), F32).ap() for i in range(2)]
    weights = (w1, w3, w2)
    with ExitStack() as ctx:
        m = Memory(nc, ctx, "c_")
        k = Constants(m, wr)
        slot_a = [m.sb("wa_hi", [P, WCOLS], F32R), m.sb("wa_lo", [P, WCOLS], F32R)]
        raw_loaded = [m.sem(f"raw_loaded{b}") for b in range(2)]
        tiles = [(m.sb(f"ntile{i}", [P, E], I32), m.sb(f"first{i}", [P, E + 1], I32)) for i in range(2)]
        attention = dict(wqT=wqT, wkT=wkT, wvT=wvT, wcT=wcT, ltriT=ltriT, wr=wr)
        with ExitStack() as early:
            raw = early.enter_context(nc.sbuf_tensor("raw1", [P, WCOLS], F32))
            route_phase(nc, k, attention, x, xn, x1, out, tables, weights, slot_a, raw, raw_loaded, tiles[0])
            expert_phase(nc, k, "e1_", xn, x1, tables[0], weights, slot_a, raw, raw_loaded, tiles[0], 2)
        middle_phase(nc, k, x1, xn, out, tables[1], tiles[1])
        with ExitStack() as late:
            raw = late.enter_context(nc.sbuf_tensor("raw2", [P, WCOLS], F32))
            expert_phase(nc, k, "e2_", xn, out, tables[1], weights, slot_a, raw, raw_loaded, tiles[1], 2 + E)


def kernel(L0_attn_X, L0_attn_Wq, L0_attn_Wk, L0_attn_Wv, L0_attn_Wc, L0_attn_Ltri,
           L0_ffn_Wr, L0_ffn_W1, L0_ffn_W3, L0_ffn_W2):
    import numpy as np
    import concourse.bacc as bacc
    from concourse.bass_utils import run_bass_kernel_spmd

    shape = np.shape(L0_attn_X)
    arrays = {
        "x": np.asarray(L0_attn_X).reshape(T, D),
        "wqT": np.asarray(L0_attn_Wq).T, "wkT": np.asarray(L0_attn_Wk).T,
        "wvT": np.asarray(L0_attn_Wv).T, "wcT": np.asarray(L0_attn_Wc).T,
        "ltriT": np.asarray(L0_attn_Ltri).transpose(0, 2, 1),
        "wr": np.asarray(L0_ffn_Wr), "w1": np.asarray(L0_ffn_W1),
        "w3": np.asarray(L0_ffn_W3), "w2": np.asarray(L0_ffn_W2),
    }
    arrays = {n: np.ascontiguousarray(a) for n, a in arrays.items()}
    nc = bacc.Bacc("TRN2", target_bir_lowering=False, num_devices=1)
    args = [nc.dram_tensor(n, a.shape, mybir.dt.from_np(a.dtype), kind="ExternalInput").ap()
            for n, a in arrays.items()]
    out = nc.dram_tensor("out", (ROWS, D), F32, kind="ExternalOutput").ap()
    macaron(nc, *args, out)
    result = run_bass_kernel_spmd(nc, [arrays], core_ids=[0])
    return result.results[0]["out"][0:T].reshape(shape)
```

```python
from contextlib import ExitStack

import concourse.bass as bass
from concourse import mybir

F32 = mybir.dt.float32
F32R = mybir.dt.float32r
BF16 = mybir.dt.bfloat16
I32 = mybir.dt.int32
U32 = mybir.dt.uint32
ALU = mybir.AluOpType
ACT = mybir.ActivationFunctionType
AX_X = mybir.AxisListType.X

P = 128
T = 4 * 2048
D = 256
KD = D // P
E = 8
TOPK = 2
F = 1024
KF = F // P
CAP = -(-T * TOPK * 5 // (4 * E))
H = 16
HD = D // H
HH = P // HD
NC = 4
GT = NC * P
G = T // GT
GB = 2048 // GT
TS = 256
TPE = CAP // TS
MIN_TILES = 2
SLOTS = E * CAP
FJ = KF // 2
WCOLS = KD * 2 * F + KF * D
W2AT = KD * 2 * F
PIECES = 12
PIECE = WCOLS // PIECES
NR = 8
GR = T // (NR * P)
ROWS = T + TS
SCOLS = SLOTS // P
EPS = 1e-5
CLAMP = 10000.0
DROPPED = 1.0e6
RSQRT_SEED = float(0x5F3759DF)
VSTEP = P + HD


def wait(eng, sem, value):
    if isinstance(value, int) and value <= 0:
        return
    eng.wait_ge(sem, value)


def wait_alone(eng, sem, value, passed):
    eng.wait_ge(sem, value)
    eng.sem_inc(passed, 1)


def mm3(pe, out, a, b, first, last):
    pe.matmul(out, a[0], b[0], start=first, stop=False)
    pe.matmul(out, a[0], b[1], start=False, stop=False)
    return pe.matmul(out, a[1], b[0], start=False, stop=last)


class Memory:

    def __init__(self, nc, ctx, prefix):
        self.nc, self.ctx, self.prefix = nc, ctx, prefix

    def sb(self, name, shape, dt=F32):
        return self.ctx.enter_context(self.nc.sbuf_tensor(self.prefix + name, shape, dt))

    def ps(self, name):
        return self.ctx.enter_context(self.nc.psum_tensor(self.prefix + name, [P, 512], F32))

    def sem(self, name):
        return self.ctx.enter_context(self.nc.semaphore(self.prefix + name))


def inverse_root(dve, y, seed, v):
    dve.tensor_scalar(seed, v.bitcast(I32), 1, None, ALU.logical_shift_right)
    dve.drain()
    dve.tensor_scalar(y.bitcast(I32), seed, -1.0, RSQRT_SEED, ALU.mult, ALU.add)
    dve.drain()
    for _ in range(3):
        s = seed.bitcast(F32)
        dve.tensor_tensor(s, y, y, ALU.mult)
        dve.drain()
        dve.scalar_tensor_tensor(s, s, -0.5, v, ALU.mult, ALU.mult)
        dve.drain()
        dve.scalar_tensor_tensor(y, s, 1.5, y, ALU.add, ALU.mult)
        dve.drain()


class Norm:

    def __init__(self, m, name, n):
        self.n = n
        self.stats = m.sb(name + "_stats", [P, n, 6])
        self.mv = m.sb(name + "_mv", [P, n, 2])
        self.var = m.sb(name + "_var", [P, n])
        self.rstd = m.sb(name + "_rstd", [P, n])
        self.seed = m.sb(name + "_seed", [P, n], I32)
        self.shift = m.sb(name + "_shift", [P, n])

    def statistics(self, dve, src, c):
        dve.bn_stats(self.stats[:, c, :], src)

    def deviation(self, dve):
        dve.drain()
        for c in range(self.n):
            dve.bn_aggr(self.mv[:, c, :], self.stats[:, c, :])
        dve.drain()
        dve.tensor_scalar(self.var[:], self.mv[:, :, 1], EPS, None, ALU.add)
        dve.drain()
        inverse_root(dve, self.rstd[:], self.seed[:], self.var[:])

    def moments(self, dve, done):
        self.deviation(dve)
        dve.scalar_tensor_tensor(self.shift[:], self.mv[:, :, 0], -1.0, self.rstd[:], ALU.mult, ALU.mult).then_inc(done, 1)

    def scaled(self, act, src, dst, done):
        for c in range(self.n):
            ins = act.activation(dst[:, c, :], src(c), ACT.Identity, scale=self.rstd[:, c:c + 1],
                                 bias=self.shift[:, c:c + 1])
            if c % 2 == 1:
                ins.then_inc(done, 1)

    def run(self, dve, src, dst, done):
        for c in range(self.n):
            self.statistics(dve, src(c), c)
        self.deviation(dve)
        for c in range(self.n):
            ins = dve.tensor_scalar(dst[:, c, :], src(c), self.mv[:, c, 0:1], self.rstd[:, c:c + 1],
                                    ALU.subtract, ALU.mult)
            if c % 2 == 1:
                ins.then_inc(done, 1)


class Router:

    def __init__(self, m, k, n, turn_banks, lg_bank, rank_bank, table, bufs, xnT=None, at=0):
        self.k, self.n, self.table = k, n, table
        self.turn_banks, self.lg_bank, self.rank_bank = turn_banks, lg_bank, rank_bank
        self.LG_AT, self.RANK_AT = at, at + n * E
        self.xnT = m.sb("r_xnT", [P, KD, n * P]) if xnT is None else xnT
        self.lg = m.sb("r_lg", [P, n, E])
        self.top = m.sb("r_top", [P, n, 8])
        self.topi = m.sb("r_topi", [P, n, 8], U32)
        self.idx = m.sb("r_idx", [P, n, TOPK])
        self.oh = m.sb("r_oh", [P, n, TOPK, E])
        self.chosen = m.sb("r_chosen", [P, n, E], BF16)
        self.diff = m.sb("r_diff", [P, n])
        self.exp = m.sb("r_exp", [P, n])
        self.den = m.sb("r_den", [P, n])
        self.prob = m.sb("r_prob", [P, n, TOPK])
        self.pos = m.sb("r_pos", [P, n, E])
        self.ohpos = m.sb("r_ohpos", [P, n, TOPK, E])
        self.slotf = m.sb("r_slotf", [P, n, TOPK])
        self.slot = m.sb("r_slot", [P, n, TOPK], I32)
        self.row = m.sb("r_row", [P, n, TOPK], I32)
        self.col = m.sb("r_col", [P, n, TOPK], I32)
        self.rank = m.sb("r_rank", [P, n, TOPK])
        self.drop = m.sb("r_drop", [P, n, TOPK])
        self.at = m.sb("r_at", [P, n, TOPK])
        self.entry = [m.sb(f"r_entry{b}", [P, n, TOPK, 2]) for b in range(bufs)]
        self.entry_at = [m.sb(f"r_entry_at{b}", [P, n, TOPK], I32) for b in range(bufs)]
        self.bufs = bufs
        self.more = m.sb("r_more", [P, E])
        self.seen = m.sb("r_seen", [P, E], BF16)
        self.xn_ready = m.sem("r_xn_ready")
        self.turned = m.sem("r_turned")
        self.xnT_ready = m.sem("r_xnT_ready")
        self.lg_made = m.sem("r_lg_made")
        self.diff_ready = m.sem("r_diff_ready")
        self.exp_ready = m.sem("r_exp_ready")
        self.chosen_ready = m.sem("r_chosen_ready")
        self.rank_made = m.sem("r_rank_made")
        self.rank_read = m.sem("r_rank_read")
        self.entry_ready = m.sem("r_entry_ready")
        self.entered = [m.sem(f"r_entered{b}") for b in range(bufs)]
        self.seen_ready = m.sem("r_seen_ready")
        self.count_made = m.sem("r_count_made")

    def start(self, dve):
        dve.memset(self.seen[:], 0.0)
        dve.drain()
        dve.nop().then_inc(self.seen_ready, 1)

    def transposes(self, pe, g, xn):
        for b in range(self.n // 2):
            pe.wait_ge(self.xn_ready, self.n // 2 * g + b + 1)
            if b >= len(self.turn_banks):
                pe.wait_ge(self.xnT_ready, self.n // 2 * g + b + 1 - len(self.turn_banks))
            bank = self.turn_banks[b % len(self.turn_banks)]
            for c in range(2):
                for h in range(KD):
                    at = (h * 2 + c) * P
                    ins = pe.transpose(bank[:, at:at + P], xn[:, 2 * b + c, h * P:(h + 1) * P], self.k.ident[:])
            ins.then_inc(self.turned, 1)

    def keep_xnT(self, act, g):
        for b in range(self.n // 2):
            act.wait_ge(self.turned, self.n // 2 * g + b + 1)
            bank = self.turn_banks[b % len(self.turn_banks)]
            act.activation(self.xnT[:, :, b * 2 * P:(b + 1) * 2 * P],
                           bank[:].rearrange("p (h t) -> p h t", h=KD), ACT.Copy).then_inc(self.xnT_ready, 1)

    def logits(self, pe, g):
        for c in range(self.n):
            if c % 2 == 0:
                pe.wait_ge(self.xnT_ready, self.n // 2 * g + c // 2 + 1)
            at = self.LG_AT + c * E
            for h in range(KD):
                ins = pe.matmul(self.lg_bank[:, at:at + E], self.xnT[:, h, c * P:(c + 1) * P], self.k.wr[:, h, :],
                                start=(h == 0), stop=(h == KD - 1))
        ins.then_inc(self.lg_made, 1)

    def choose(self, dve, g):
        n = self.n
        dve.wait_ge(self.lg_made, g + 1)
        dve.tensor_scalar(self.lg[:], self.lg_bank[:, self.LG_AT:self.LG_AT + n * E].rearrange("p (c e) -> p c e", c=n),
                          -CLAMP, CLAMP, ALU.max, ALU.min)
        dve.drain()
        for c in range(n):
            dve.max(self.top[:, c, :], self.lg[:, c, :])
        dve.drain()
        dve.tensor_tensor(self.diff[:], self.top[:, :, 1], self.top[:, :, 0], ALU.subtract).then_inc(self.diff_ready, 1)
        for c in range(n):
            dve.max_index(self.topi[:, c, :], self.top[:, c, :], self.lg[:, c, :])
        dve.drain()
        dve.tensor_copy(self.idx[:], self.topi[:, :, 0:TOPK])
        dve.drain()
        dve.tensor_tensor(self.oh[:], self.k.expert[:].unsqueeze(1).unsqueeze(1).broadcast_to([P, n, TOPK, E]),
                          self.idx[:].unsqueeze(3).broadcast_to([P, n, TOPK, E]), ALU.is_equal)
        dve.drain()
        dve.tensor_tensor(self.chosen[:], self.oh[:, :, 0, :], self.oh[:, :, 1, :],
                          ALU.add).then_inc(self.chosen_ready, 1)

    def weigh(self, act, g):
        act.wait_ge(self.diff_ready, g + 1)
        act.activation(self.exp[:], self.diff[:], ACT.Exp).then_inc(self.exp_ready, 1)

    def rank_out(self):
        return self.rank_bank[:, self.RANK_AT:self.RANK_AT + self.n * E].rearrange("p (c e) -> p c e", c=self.n)

    def ranks(self, pe, g):
        n, out = self.n, self.rank_out()
        pe.wait_ge(self.chosen_ready, g + 1)
        pe.wait_ge(self.seen_ready, g + 1)
        pe.matmul(out, self.k.before[:], self.chosen[:], start=True, stop=False)
        for c in range(1, n):
            pe.matmul(out[:, c:n, :], self.k.ones[:],
                      self.chosen[:, c - 1:c, :].broadcast_to([P, n - c, E]), start=False, stop=False)
        pe.matmul(out, self.k.ones[:], self.seen[:].unsqueeze(1).broadcast_to([P, n, E]),
                  start=False, stop=True).then_inc(self.rank_made, 1)

    def place(self, dve, g, b, entered):
        self.place_first(dve, g)
        self.place_rest(dve, g, b, entered)

    def place_first(self, dve, g):
        n = self.n
        dve.wait_ge(self.rank_made, g + 1)
        dve.tensor_tensor(self.pos[:], self.rank_out(),
                          self.k.region[:].unsqueeze(1).broadcast_to([P, n, E]), ALU.add).then_inc(self.rank_read, 1)
        dve.tensor_reduce(self.more[:], self.chosen[:].rearrange("p c e -> p e c"), AX_X, ALU.add)
        dve.drain()
        dve.tensor_tensor(self.seen[:], self.seen[:], self.more[:], ALU.add).then_inc(self.seen_ready, 1)
        dve.tensor_tensor(self.ohpos[:], self.oh[:], self.pos[:].unsqueeze(2).broadcast_to([P, n, TOPK, E]), ALU.mult)
        dve.wait_ge(self.exp_ready, g + 1)
        dve.tensor_scalar(self.den[:], self.exp[:], 1.0, 1e-12, ALU.add, ALU.add)
        dve.drain()
        dve.tensor_reduce(self.slotf[:], self.ohpos[:], AX_X, ALU.add)
        dve.reciprocal(self.prob[:, :, 0], self.den[:])
        dve.drain()

    def place_rest(self, dve, g, b, entered):
        n, entry, entry_at = self.n, self.entry[b], self.entry_at[b]
        dve.tensor_copy(self.slot[:], self.slotf[:])
        dve.scalar_tensor_tensor(self.rank[:], self.idx[:], -float(CAP), self.slotf[:], ALU.mult, ALU.add)
        dve.tensor_tensor(self.prob[:, :, 1], self.exp[:], self.prob[:, :, 0], ALU.mult)
        dve.drain()
        dve.tensor_scalar(self.row[:], self.slot[:], P - 1, None, ALU.bitwise_and)
        dve.tensor_scalar(self.col[:], self.slot[:], P.bit_length() - 1, None, ALU.logical_shift_right)
        dve.tensor_scalar(self.drop[:], self.rank[:], float(CAP), DROPPED, ALU.is_ge, ALU.mult)
        dve.drain()
        dve.scalar_tensor_tensor(self.at[:], self.row[:], float(SCOLS), self.col[:], ALU.mult, ALU.add)
        wait(dve, self.entered[b], entered)
        token = self.k.token[:].rearrange("p (g c) -> p g c", c=n)
        token = token[:, g] if isinstance(g, int) else token[:, bass.ds(g, 1)].rearrange("p o c -> p (o c)")
        dve.tensor_copy(entry[:, :, :, 0].bitcast(I32), token.unsqueeze(2).broadcast_to([P, n, TOPK]))
        dve.tensor_scalar(entry[:, :, :, 1], self.prob[:], 0.5, None, ALU.mult)
        dve.drain()
        dve.tensor_tensor(entry_at[:], self.at[:], self.drop[:], ALU.add).then_inc(self.entry_ready, 1)

    def enter(self, pool, g, b):
        wait_alone(pool, self.entry_ready, g + 1, self.k.passed)
        for c in range(self.n):
            for j in range(TOPK):
                pool.indirect_dma_start(
                    self.table, bass.IndirectOffsetOnAxis(ap=self.entry_at[b][:, c, j:j + 1], axis=0),
                    self.entry[b][:, c, j, :], None,
                    bounds_check=SLOTS - 1, oob_is_err=False).then_inc(self.entered[b], 16)

    def count(self, pe, groups):
        pe.wait_ge(self.seen_ready, groups + 1)
        pe.wait_ge(self.rank_read, groups)
        pe.matmul(self.rank_bank[:, self.RANK_AT:self.RANK_AT + E], self.k.ones[:], self.seen[:], start=True, stop=True).then_inc(self.count_made, 1)

    def tiles(self, dve, ntile, first_tile):
        cnt, cnti, scan, zero = self.lg[:, 0, :], self.topi[:, 0, :].bitcast(I32), self.lg[:, 1, :], self.lg[:, 2, :]
        dve.wait_ge(self.count_made, 1)
        dve.tensor_scalar(cnt, self.rank_bank[:, self.RANK_AT:self.RANK_AT + E], float(CAP), float(TS - 1), ALU.min, ALU.add)
        dve.memset(zero, 0.0)
        dve.drain()
        dve.tensor_copy(cnti, cnt)
        dve.drain()
        dve.tensor_scalar(cnti, cnti, TS.bit_length() - 1, None, ALU.logical_shift_right)
        dve.drain()
        dve.tensor_scalar(cnt, cnti, float(MIN_TILES), None, ALU.max)
        dve.drain()
        dve.tensor_copy(ntile[:], cnt)
        dve.tensor_tensor_scan(scan, cnt, zero, 0.0, ALU.add, ALU.add)
        dve.memset(first_tile[:, 0:1], 0.0)
        dve.drain()
        dve.tensor_copy(first_tile[:, 1:E + 1], scan)


class Setup:

    def __init__(self, m, k, inputs, bank_b, bank_m):
        self.k, self.inputs, self.pb, self.pm = k, inputs, bank_b, bank_m
        self.raw_qk = m.sb("su_raw_qk", [P, KD, 2 * D])
        self.raw_v = m.sb("su_raw_v", [P, KD, D])
        self.wc = m.sb("su_wc", [P, KD, D])
        self.lt = m.sb("su_lt", [P, KD, HD])
        self.low = m.sb("su_low", [P, P])
        self.lbd = m.sb("su_lbd", [P, KD, P])
        self.bbd = m.sb("su_bbd", [P, KD, P])
        self.wr_loaded, self.loads = m.sem("su_wr_loaded"), m.sem("su_loads")
        self.masks0, self.masks = m.sem("su_masks0"), m.sem("su_masks")
        self.split, self.tri_ready = m.sem("su_split"), m.sem("su_tri_ready")
        self.bbd_made, self.bbd_ready = m.sem("su_bbd_made"), m.sem("su_bbd_ready")
        self.fold_made = m.sem("su_fold_made")

    def load_router(self, q):
        q.dma_start(self.k.wr[:], self.inputs["wr"].rearrange("(k p) n -> p k n", p=P)).then_inc(self.wr_loaded, 16)

    def load(self, q):
        inputs, loads = self.inputs, self.loads

        def by_k(w):
            return w.rearrange("(k p) n -> p k n", p=P)

        q.dma_start(self.raw_qk[:, :, 0:D], by_k(inputs["wqT"])).then_inc(loads, 16)
        q.dma_start(self.raw_qk[:, :, D:2 * D], by_k(inputs["wkT"])).then_inc(loads, 16)
        q.dma_start(self.raw_v[:], by_k(inputs["wvT"])).then_inc(loads, 16)
        q.dma_start(self.wc[:], by_k(inputs["wcT"])).then_inc(loads, 16)
        q.dma_start(self.lt[:], inputs["ltriT"].rearrange("(a h) k e -> (h k) a e", a=KD)).then_inc(loads, 16)

    def make_masks(self, pool):
        k, masks0 = self.k, self.masks0
        pool.memset(k.ident[:], 0.0)
        pool.memset(k.before[:], 1.0)
        pool.memset(k.causal[:], 1.0)
        pool.memset(k.heads[:], 1.0)
        pool.iota(k.expert_i[:], pattern=[[1, E]], base=0, channel_multiplier=0)
        pool.iota(k.region_i[:], pattern=[[CAP, E]], base=0, channel_multiplier=0)
        pool.iota(k.later_i[:], pattern=[[0, G // GB], [1, GB]], base=0, channel_multiplier=0)
        pool.iota(k.token[:], pattern=[[P, T // P]], base=0, channel_multiplier=1)
        pool.iota(k.spare[:], pattern=[[P, TS // P]], base=T, channel_multiplier=1)
        pool.memset(k.ones[:], 1.0).then_inc(masks0, 1)
        pool.wait_ge(masks0, 1)
        pool.affine_select(out=k.ident[:], in_=k.ident[:], compare_op=ALU.not_equal, fill=1.0,
                           base=0, pattern=[[-1, P]], channel_multiplier=1)
        pool.affine_select(out=k.before[:], in_=k.before[:], compare_op=ALU.is_ge, fill=0.0,
                           base=-1, pattern=[[1, P]], channel_multiplier=-1)
        pool.affine_select(out=k.causal[:], in_=k.causal[:], compare_op=ALU.is_ge, fill=0.0,
                           base=0, pattern=[[1, P]], channel_multiplier=-1)
        pool.affine_select(out=k.heads[:], in_=k.heads[:], compare_op=ALU.is_ge, fill=0.0,
                           base=0, pattern=[[-HD, HH]], channel_multiplier=1).then_inc(masks0, 1)
        pool.wait_ge(masks0, 2)
        pool.affine_select(out=k.heads[:], in_=k.heads[:], compare_op=ALU.is_ge, fill=0.0,
                           base=HD - 1, pattern=[[HD, HH]], channel_multiplier=-1).then_inc(masks0, 1)
        pool.wait_ge(masks0, 3)
        pool.tensor_copy(k.same_head[:].rearrange("p (h e) -> p h e", e=HD),
                         k.heads[:].unsqueeze(2).broadcast_to([P, HH, HD])).then_inc(self.masks, 1)

    def numbers(self, dve):
        k = self.k
        dve.wait_ge(self.masks0, 1)
        dve.tensor_copy(k.expert[:], k.expert_i[:])
        dve.tensor_copy(k.region[:], k.region_i[:])
        dve.tensor_scalar(k.later[:], k.later_i[:].rearrange("p a b -> p (a b)"), 0.5, None, ALU.is_gt)

    def spread_tri(self, dve):
        k = self.k
        dve.wait_ge(self.masks, 1)
        dve.tensor_tensor(self.low[:], k.causal[:], k.same_head[:], ALU.mult)
        dve.drain()
        dve.wait_ge(self.loads, 16 * 5)
        for a in range(KD):
            dve.tensor_tensor(self.lbd[:, a, :].rearrange("p (h e) -> p h e", e=HD),
                              self.low[:].rearrange("p (h e) -> p h e", e=HD),
                              self.lt[:, a, :].unsqueeze(1).broadcast_to([P, HH, HD]),
                              ALU.mult).then_inc(self.tri_ready, 1)

    def low_parts(self, dve):
        k = self.k
        dve.wait_ge(self.split, 2)
        dve.tensor_tensor(k.wqk[1][:], self.raw_qk[:], k.wqk[0][:].bitcast(F32), ALU.subtract)
        dve.tensor_tensor(k.wv[1][:], self.raw_v[:], k.wv[0][:].bitcast(F32), ALU.subtract)
        dve.wait_ge(self.split, 3)
        dve.tensor_tensor(k.fold[1][:].rearrange("p a n -> p (a n)"), self.pm[:],
                          k.fold[0][:].bitcast(F32).rearrange("p a n -> p (a n)"), ALU.subtract)

    def high_parts(self, act):
        k = self.k
        act.wait_ge(self.loads, 16 * 5)
        act.activation(k.wqk[0][:], self.raw_qk[:], ACT.Copy).then_inc(self.split, 1)
        act.activation(k.wv[0][:], self.raw_v[:], ACT.Copy).then_inc(self.split, 1)
        act.wait_ge(self.bbd_made, 1)
        act.activation(self.bbd[:], self.pb[:, 0:KD * P].rearrange("p (a n) -> p a n", a=KD),
                       ACT.Copy).then_inc(self.bbd_ready, 1)
        act.wait_ge(self.fold_made, 1)
        act.activation(k.fold[0][:], self.pm[:].rearrange("p (a n) -> p a n", a=KD), ACT.Copy).then_inc(self.split, 1)

    def fold_heads(self, pe):
        pe.wait_ge(self.tri_ready, KD)
        for a in range(KD):
            ins = pe.matmul(self.pb[:, a * P:(a + 1) * P], self.lbd[:, a, :], self.lbd[:, a, :], start=True, stop=True)
        ins.then_inc(self.bbd_made, 1)
        pe.wait_ge(self.bbd_ready, 1)
        for a in range(KD):
            ins = pe.matmul(self.pm[:, a * D:(a + 1) * D], self.bbd[:, a, :], self.wc[:, a, :], start=True, stop=True)
        ins.then_inc(self.fold_made, 1)


def piece(t, q):
    return t[:, q * PIECE:(q + 1) * PIECE]


def load_expert(sp, w, e, raw, raw_loaded, n):
    w1, w3, w2 = w
    pick = (lambda t: t[e]) if isinstance(e, int) else (lambda t: t[bass.ds(e, 1)].rearrange("o a b -> (o a) b"))
    for q in range(PIECES):
        wait(sp, raw_loaded[q % 2], 16 * (PIECES // 2 * n + q // 2))
        if q * PIECE < W2AT:
            kk, col = divmod(q * PIECE, 2 * F)
            src = pick(w1 if col < F else w3)[kk * P:(kk + 1) * P, col % F:col % F + PIECE]
            dst = piece(raw, q)
        else:
            row = (q * PIECE - W2AT) // D * P
            src = pick(w2)[row:row + PIECE // D * P, :].rearrange("(k p) d -> p k d", p=P)
            dst = piece(raw, q).rearrange("p (k d) -> p k d", d=D)
        sp.dma_start(dst, src).then_inc(raw_loaded[q % 2], 16)


def wait_raw(eng, raw_loaded, n, q=None):
    if q is None:
        for b in range(2):
            eng.wait_ge(raw_loaded[b], 16 * (PIECES // 2) * (n + 1))
    else:
        eng.wait_ge(raw_loaded[q % 2], 16 * (PIECES // 2 * n + q // 2 + 1))


def route_phase(nc, k, attention, x_in, xn_out, x1_out, out, tables, w, slot_a, raw, raw_loaded, tiles_out):
    ntile, first_tile = tiles_out
    with ExitStack() as ctx:
        m = Memory(nc, ctx, "r1_")
        xin = [m.sb(f"xin{s}", [P, NR, D]) for s in range(2)]
        xn = [m.sb(f"xn{s}", [P, NR, D]) for s in range(2)]
        zeros = m.sb("zeros", [P, D])
        unfilled = m.sb("unfilled", [P, SCOLS, 2])
        turn_banks = [m.ps(f"turn{i}") for i in range(4)]
        r = Router(m, k, NR, turn_banks, m.ps("lg"), m.ps("rank"), tables[0], 2)
        norm = Norm(m, "n", NR)
        su = Setup(m, k, attention, m.ps("pb"), m.ps("pm"))
        x_loaded = [m.sem(f"x_loaded{s}") for s in range(2)]
        x_copied = [m.sem(f"x_copied{s}") for s in range(2)]
        xn_stored = [m.sem(f"xn_stored{s}") for s in range(2)]
        w_high = m.sem("w_high")
        w_low = m.sem("w_low")
        blank = m.sem("blank")
        cleared = m.sem("cleared")

        x_g, x1_g, xn_g = (t[0:T, :].rearrange("(g c p) d -> g p c d", p=P, c=NR) for t in (x_in, x1_out, xn_out))

        def group(t, g):
            return t[g] if isinstance(g, int) else t[bass.ds(g, 1)].rearrange("o p c d -> p (o c) d")

        def rounds(eng, step):
            for s in range(2):
                step(s, s, 0)
            with eng.Fori(1, GR // 2) as i:
                for s in range(2):
                    step(2 * i + s, s, i)

        with nc.Block() as block:
            @block.sync
            def _(sp):
                def load(g, s):
                    sp.dma_start(xin[s][:], group(x_g, g)).then_inc(x_loaded[s], 16)

                def next_load(i, s):
                    sp.wait_ge(r.xn_ready, NR // 2 * (2 * i + s + 1))
                    sp.wait_ge(x_copied[s], 16 * i + 16)
                    load(2 * i + s + 2, s)

                load(0, 0)
                su.load_router(sp)
                load(1, 1)
                su.load(sp)
                for s in range(2):
                    next_load(0, s)
                load_expert(sp, w, 0, raw, raw_loaded, 0)
                with sp.Fori(1, GR // 2 - 1) as i:
                    for s in range(2):
                        next_load(i, s)
                sp.wait_ge(w_low, 1)
                load_expert(sp, w, 1, raw, raw_loaded, 1)
                wait_raw(sp, raw_loaded, 1)

            @block.scalar
            def _(act):
                act.wait_ge(blank, 1)
                for i in range(2):
                    act.dma_start(tables[i].rearrange("(p n) c -> p (n c)", p=P),
                                  unfilled[:].rearrange("p n c -> p (n c)")).then_inc(cleared, 16)
                for t in (xn_out, x1_out, out):
                    act.dma_start(t[T:ROWS, :].rearrange("(r p) d -> p r d", p=P),
                                  zeros[:].unsqueeze(1).broadcast_to([P, TS // P, D])).then_inc(cleared, 16)

                def step(g, s, i):
                    act.wait_ge(x_loaded[s], 16 * i + 16)
                    act.dma_start(group(x1_g, g), xin[s][:]).then_inc(x_copied[s], 16)
                    r.keep_xnT(act, g)
                    act.dma_start(group(xn_g, g), xn[s][:]).then_inc(xn_stored[s], 16)
                    r.weigh(act, g)
                    if isinstance(g, int) and g == 0:
                        su.high_parts(act)

                rounds(act, step)
                wait_raw(act, raw_loaded, 0)
                act.activation(slot_a[0][:], raw[:], ACT.Copy).then_inc(w_high, 1)
                act.wait_ge(cleared, 16 * 5)
                for s in range(2):
                    act.wait_ge(x_copied[s], 16 * (GR // 2))
                    act.wait_ge(xn_stored[s], 16 * (GR // 2))

            @block.vector
            def _(dve):
                def ln(g, s, i):
                    dve.wait_ge(x_loaded[s], 16 * (i + 1))
                    wait(dve, xn_stored[s], 16 * i)
                    norm.run(dve, lambda c: xin[s][:, c, :], xn[s], r.xn_ready)

                def step(g, s, i, last=False):
                    r.choose(dve, g)
                    r.place(dve, g, s, 16 * NR * TOPK * i)
                    if not last:
                        ln(g + 2, s, i + 1)
                    if isinstance(g, int) and g == 0:
                        su.low_parts(dve)

                su.numbers(dve)
                dve.memset(zeros[:], 0.0)
                dve.memset(unfilled[:], 0.0)
                dve.drain()
                dve.tensor_copy(unfilled[:].rearrange("p (n s) c -> p n s c", s=TS // P)[:, :, :, 0].bitcast(I32),
                                k.spare[:].unsqueeze(1).broadcast_to([P, SCOLS * P // TS, TS // P])).then_inc(blank, 1)
                r.start(dve)
                ln(0, 0, 0)
                ln(1, 1, 0)
                su.spread_tri(dve)
                step(0, 0, 0)
                step(1, 1, 0)
                with dve.Fori(1, GR // 2 - 1) as i:
                    for s in range(2):
                        step(2 * i + s, s, i)
                step(GR - 2, 0, GR // 2 - 1, last=True)
                step(GR - 1, 1, GR // 2 - 1, last=True)
                dve.wait_ge(w_high, 1)
                dve.tensor_tensor(slot_a[1][:], raw[:], slot_a[0][:].bitcast(F32), ALU.subtract).then_inc(w_low, 1)
                r.tiles(dve, ntile, first_tile)

            @block.gpsimd
            def _(pool):
                su.make_masks(pool)
                pool.wait_ge(cleared, 16 * 5)
                rounds(pool, lambda g, s, i: r.enter(pool, g, s))
                for s in range(2):
                    pool.wait_ge(r.entered[s], 16 * NR * TOPK * (GR // 2))

            @block.tensor
            def _(pe):
                def step(g, s, i):
                    r.transposes(pe, g, xn[s])
                    wait(pe, r.chosen_ready, g)
                    r.logits(pe, g)
                    wait(pe, r.rank_read, g)
                    r.ranks(pe, g)

                pe.wait_ge(su.masks, 1)
                pe.wait_ge(su.wr_loaded, 16)
                step(0, 0, 0)
                su.fold_heads(pe)
                step(1, 1, 0)
                with pe.Fori(1, GR // 2) as i:
                    for s in range(2):
                        step(2 * i + s, s, i)
                r.count(pe, GR)


def expert_phase(nc, k, name, xn, acc, table, w, slot_a, raw, raw_loaded, tiles, loaded):
    ntile, first_tile = tiles
    with ExitStack() as ctx:
        m = Memory(nc, ctx, name)
        slot_b = [m.sb("wb_hi", [P, WCOLS], F32R), m.sb("wb_lo", [P, WCOLS], F32R)]
        slots = [slot_a, slot_b]
        entries = m.sb("entries", [P, E * TPE, TS // P, 2])
        token = m.sb("token", [P, 2], I32)
        held_token = m.sb("held_token", [P, 2], I32)
        held_weight = m.sb("held_weight", [P, 2])
        y_token = m.sb("y_token", [P, 2], I32)
        y_weight = m.sb("y_weight", [P, 2])
        xrow = m.sb("xrow", [P, 2, D])
        xT = [m.sb("xT_hi", [P, KD, TS], F32R), m.sb("xT_lo", [P, KD, TS], F32R)]
        gate = m.sb("gate", [P, 2, 512])
        hid = m.sb("hid", [P, 2, 512])
        h = [m.sb("h_hi", [P, KF * TS], F32R), m.sb("h_lo", [P, KF * TS], F32R)]
        yrow = m.sb("yrow", [P, 2, D])
        ps1 = [m.ps(f"ps1_{b}") for b in range(2)]
        ps3 = [m.ps(f"ps3_{b}") for b in range(2)]
        psx = m.ps("psx")
        psy = m.ctx.enter_context(nc.psum_tensor(name + "psy", [P, 2, 512], F32))

        entries_loaded = m.sem("entries_loaded")
        token_ready = m.sem("token_ready")
        held = m.sem("held")
        y_meta = m.sem("y_meta")
        x_loaded = m.sem("x_loaded")
        x_turned = m.sem("x_turned")
        x_high = m.sem("x_high")
        x_ready = m.sem("x_ready")
        h_made = m.sem("h_made")
        gated = m.sem("gated")
        hid_ready = m.sem("hid_ready")
        h_high = m.sem("h_high")
        h_ready = m.sem("h_ready")
        y_made = m.sem("y_made")
        y_kept = m.sem("y_kept")
        y_added = m.sem("y_added")
        w_high = m.sem("w_high")
        w_low = m.sem("w_low")

        def experts(eng, tile_body):
            with eng.Fori(0, E // 2) as i:
                for s in range(2):
                    e = i * 2 + s
                    f = eng.value_load(first_tile[0:1, bass.ds(e, 1)], min_val=0, max_val=E * TPE)
                    n = eng.value_load(ntile[0:1, bass.ds(e, 1)], min_val=MIN_TILES, max_val=TPE)
                    tile_body(e, s, 0, f)
                    with eng.Fori(1, n) as t:
                        tile_body(e, s, t, eng.snap(f + t))

        def total(eng):
            return eng.value_load(first_tile[0:1, E:E + 1], min_val=MIN_TILES * E, max_val=E * TPE)

        def first_of(t):
            return isinstance(t, int)

        with nc.Block() as block:
            @block.sync
            def _(sp):
                sp.dma_start(entries[:].rearrange("p n s c -> p (n s c)"),
                             table.rearrange("(p n) c -> p (n c)", p=P)).then_inc(entries_loaded, 16)
                if loaded > 2:
                    load_expert(sp, w, 1, raw, raw_loaded, loaded - 1)
                with sp.Fori(0, E - 2) as e:
                    sp.wait_ge(w_low, PIECES * (e + 2))
                    load_expert(sp, w, e + 2, raw, raw_loaded, e + loaded)
                sp.wait_ge(w_low, PIECES * E)
                load_expert(sp, w, 0, raw, raw_loaded, loaded + E - 2)
                wait_raw(sp, raw_loaded, loaded + E - 2)

            @block.gpsimd
            def _(pool):
                def gather():
                    for sub in range(2):
                        pool.indirect_dma_start(
                            xrow[:, sub, :], None, xn,
                            bass.IndirectOffsetOnAxis(ap=token[:, sub:sub + 1], axis=0),
                            bounds_check=ROWS - 1, oob_is_err=True).then_inc(x_loaded, 16)

                def add():
                    for sub in range(2):
                        pool.indirect_dma_start(
                            acc, bass.IndirectOffsetOnAxis(ap=y_token[:, sub:sub + 1], axis=0),
                            yrow[:, sub, :], None, bounds_check=ROWS - 1, oob_is_err=True,
                            compute_op=ALU.add).then_inc(y_added, 16)

                def hold(at):
                    pool.tensor_copy(held_weight[:], entries[:, at, :, 1].rearrange("p o s -> p (o s)"))
                    pool.tensor_copy(held_token[:], entries[:, at, :, 0].rearrange("p o s -> p (o s)").bitcast(I32)
                                     ).then_inc(held, 1)

                def add_last(g):
                    pool.wait_ge(y_added, 32 * g + 32)
                    wait_alone(pool, held, g + 1, k.passed)
                    pool.tensor_copy(y_weight[:], held_weight[:])
                    pool.tensor_copy(y_token[:], held_token[:]).then_inc(y_meta, 1)

                def tile(e, s, t, g):
                    at = bass.ds(e * TPE + t, 1)
                    wait_alone(pool, x_turned, g + 1, k.passed)
                    pool.tensor_copy(token[:], entries[:, at, :, 0].rearrange("p o s -> p (o s)").bitcast(I32)
                                     ).then_inc(token_ready, 1)
                    wait_alone(pool, token_ready, g + 1, k.passed)
                    gather()
                    add_last(g)
                    wait_alone(pool, y_meta, g + 1, k.passed)
                    hold(at)
                    wait_alone(pool, y_kept, g + 1, k.passed)
                    add()

                pool.memset(yrow[:], 0.0)
                pool.memset(held_weight[:], 0.0)
                pool.tensor_copy(held_token[:], k.spare[:])
                pool.tensor_copy(y_token[:], k.spare[:]).then_inc(held, 1)
                pool.nop().then_inc(y_kept, 1)
                wait_alone(pool, held, 1, k.passed)
                add()
                pool.wait_ge(entries_loaded, 16)
                experts(pool, tile)
                n = total(pool)
                wait_alone(pool, x_turned, n + 1, k.passed)
                gather()
                add_last(n)
                wait_alone(pool, y_meta, n + 1, k.passed)
                wait_alone(pool, y_kept, n + 1, k.passed)
                add()
                wait_alone(pool, y_added, 32 * n + 64, k.passed)
                wait_alone(pool, x_loaded, 32 * n + 32, k.passed)

            @block.tensor
            def _(pe):
                pe.nop().then_inc(x_turned, 1)
                pe.nop().then_inc(y_made, 1)

                def turn(n_loaded):
                    pe.wait_ge(x_loaded, n_loaded)
                    for half in range(KD):
                        for sub in range(2):
                            at = half * TS + sub * P
                            ins = pe.transpose(psx[:, at:at + P], xrow[:, sub, half * P:(half + 1) * P], k.ident[:])
                    ins.then_inc(x_turned, 1)

                def tile(e, s, t, g):
                    hi, lo = slots[s]

                    def wt(at):
                        return hi[:, at:at + P], lo[:, at:at + P]

                    def w2t(f):
                        at = W2AT + f * D
                        return hi[:, at:at + D], lo[:, at:at + D]

                    if first_of(t):
                        pe.wait_ge(w_low, PIECES * (e + 1))
                    pe.wait_ge(x_ready, g + 1)
                    for j in range(FJ):
                        pe.wait_ge(hid_ready, 4 * g + j + 1)
                        for fi in range(2):
                            f = 2 * j + fi
                            for ps, base in ((ps1[j % 2], 0), (ps3[j % 2], F)):
                                for kk in range(KD):
                                    ins = mm3(pe, ps[:, fi * TS:(fi + 1) * TS], wt(kk * 2 * F + base + f * P),
                                              (xT[0][:, kk, :], xT[1][:, kk, :]), kk == 0, kk == KD - 1)
                        ins.then_inc(h_made, 1)
                    turn(32 * g + 64)
                    pe.wait_ge(y_kept, g + 1)
                    for j in range(FJ):
                        pe.wait_ge(h_ready, 4 * g + j + 1)
                        for fi in range(2):
                            f = 2 * j + fi
                            for sub in range(2):
                                at = f * TS + sub * P
                                ins = mm3(pe, psy[:, sub, 0:D], (h[0][:, at:at + P], h[1][:, at:at + P]), w2t(f),
                                          f == 0, f == KF - 1)
                    ins.then_inc(y_made, 1)

                turn(32)
                experts(pe, tile)

            with_pair = (range(0, 2), range(2, 4), range(4, 5), range(5, 5))
            before_y, behind_y = range(5, 9), range(9, PIECES)

            @block.scalar
            def _(act):
                def high_w(e, s, q):
                    wait_raw(act, raw_loaded, e + loaded - 1, q)
                    act.activation(piece(slots[1 - s][0], q), piece(raw, q), ACT.Copy).then_inc(w_high, 1)

                def high_x(n):
                    act.wait_ge(x_turned, n)
                    act.activation(xT[0][:], psx[:].rearrange("p (k t) -> p k t", k=KD), ACT.Copy).then_inc(x_high, 1)

                def tile(e, s, t, g):
                    if first_of(t):
                        act.wait_ge(y_made, g + 1)
                    for j in range(FJ):
                        act.wait_ge(h_made, 4 * g + j + 1)
                        act.wait_ge(hid_ready, 4 * g + j + 1)
                        act.activation(gate[:, j % 2, :], ps1[j % 2][:], ACT.Silu).then_inc(gated, 1)
                        act.wait_ge(hid_ready, 4 * g + j + 3)
                        act.activation(h[0][:, j * 512:(j + 1) * 512], hid[:, j % 2, :], ACT.Copy).then_inc(h_high, 1)
                        if first_of(t):
                            for q in with_pair[j]:
                                high_w(e, s, q)
                    high_x(g + 3)
                    if first_of(t):
                        for q in before_y:
                            high_w(e, s, q)
                    act.wait_ge(y_made, g + 2)
                    act.wait_ge(y_meta, g + 2)
                    for sub in range(2):
                        ins = act.activation(yrow[:, sub, :], psy[:, sub, 0:D], ACT.Copy, scale=y_weight[:, sub:sub + 1])
                    ins.then_inc(y_kept, 1)
                    if first_of(t):
                        for q in behind_y:
                            high_w(e, s, q)

                high_x(2)
                experts(act, tile)

            @block.vector
            def _(dve):
                dve.nop().then_inc(hid_ready, 2)
                dve.nop().then_inc(w_low, PIECES)

                def low_w(e, s, q):
                    dve.wait_ge(w_high, PIECES * e + q + 1)
                    dve.tensor_tensor(piece(slots[1 - s][1], q), piece(raw, q), piece(slots[1 - s][0], q).bitcast(F32),
                                      ALU.subtract).then_inc(w_low, 1)

                def low_x(n):
                    dve.wait_ge(x_high, n)
                    dve.tensor_tensor(xT[1][:], psx[:].rearrange("p (k t) -> p k t", k=KD), xT[0][:].bitcast(F32),
                                      ALU.subtract).then_inc(x_ready, 1)

                def tile(e, s, t, g):
                    for j in range(FJ):
                        dve.wait_ge(gated, 4 * g + j + 1)
                        dve.tensor_tensor(hid[:, j % 2, :], ps3[j % 2][:], gate[:, j % 2, :],
                                          ALU.mult).then_inc(hid_ready, 1)
                        dve.wait_ge(h_high, 4 * g + j + 1)
                        at = slice(j * 512, (j + 1) * 512)
                        dve.tensor_tensor(h[1][:, at], hid[:, j % 2, :], h[0][:, at].bitcast(F32),
                                          ALU.subtract).then_inc(h_ready, 1)
                        if first_of(t):
                            for q in with_pair[j]:
                                low_w(e, s, q)
                    low_x(g + 2)
                    if first_of(t):
                        for q in range(before_y[0], PIECES):
                            low_w(e, s, q)

                low_x(1)
                experts(dve, tile)


def middle_phase(nc, k, x1_in, xn_out, x2_out, table, tiles_out):
    ntile, first_tile = tiles_out
    with ExitStack() as ctx:
        m = Memory(nc, ctx, "mi_")
        x1 = m.sb("x1", [P, 2, NC, D])
        x2 = m.sb("x2", [P, 2, NC, D])
        shared = m.sb("xn", [P, NC * D])
        xn = shared[:].rearrange("p (c d) -> p c d", c=NC)
        xT = [m.sb("xT_hi", [P, KD, GT], F32R), m.sb("xT_lo", [P, KD, GT], F32R)]
        qT = m.sb("qT", [P, KD, GT])
        qkT = [m.sb("qkT_hi", [P, 2 * KD, GT], F32R), m.sb("qkT_lo", [P, 2 * KD, GT], F32R)]
        qx = [[m.sb(f"qx{b}_{part}", [P, KD, HH, P], F32R) for part in ("hi", "lo")] for b in range(2)]
        vpad = [m.sb(f"vpad{b}", [P, KD * HH * P + P]) for b in range(2)]
        kT = m.sb("kT", [P, KD, GT])
        krow = [m.sb(f"krow{b}", [P, D]) for b in range(2)]
        prob = [m.sb(f"prob{b}", [P, H, P]) for b in range(2)]
        state = [m.sb(f"state{b}", [P, KD, P]) for b in range(2)]
        update = m.sb("update", [P, KD, P])
        yT = [m.sb("yT_hi", [P, KD, P], F32R), m.sb("yT_lo", [P, KD, P], F32R)]
        xn2 = m.sb("xn2", [P, NC, D])
        sc = [m.ps("sc0"), m.ps("sc1")]
        wide = [m.ps("wide0"), m.ps("wide1")]
        vk, yt, kv, op = m.ps("vk"), m.ps("yt"), m.ps("kv"), m.ps("op")
        norm1, norm2 = Norm(m, "n1", NC), Norm(m, "n2", NC)
        r = Router(m, k, NC, wide, op, op, table, 2, xnT=shared[:].rearrange("p (h t) -> p h t", h=KD), at=D)

        x_loaded = m.sem("x_loaded")
        norm1_ready = m.sem("norm1_ready")
        xn_ready = m.sem("xn_ready")
        norm2_ready = m.sem("norm2_ready")
        turned = m.sem("turned")
        x_high = m.sem("x_high")
        xT_ready = m.sem("xT_ready")
        qk_made = m.sem("qk_made")
        qk_kept = m.sem("qk_kept")
        qk_high = m.sem("qk_high")
        qk_low = m.sem("qk_low")
        qx_ready = m.sem("qx_ready")
        vk_made = m.sem("vk_made")
        vk_kept = m.sem("vk_kept")
        sc_made = m.sem("sc_made")
        prob_ready = m.sem("prob_ready")
        kv_made = m.sem("kv_made")
        state_ready = m.sem("state_ready")
        fresh = m.sem("fresh")
        y_made = m.sem("y_made")
        y_high = m.sem("y_high")
        y_ready = m.sem("y_ready")
        o_made = m.sem("o_made")
        x2_ready = m.sem("x2_ready")
        x2_stored = [m.sem(f"x2_stored{s}") for s in range(2)]
        xn2_stored = m.sem("xn2_stored")
        vzero = m.sem("vzero")

        x1_g, x2_g, xn_g = (t[0:T, :].rearrange("(g c p) d -> g p c d", p=P, c=NC) for t in (x1_in, x2_out, xn_out))

        def group(t, g):
            return t[g] if isinstance(g, int) else t[bass.ds(g, 1)].rearrange("o p c d -> p (o c) d")

        def rounds(eng, step):
            step(0, 0, True, False)
            step(1, 1, False, False)
            with eng.Fori(1, G // 2 - 1) as i:
                for s in range(2):
                    step(2 * i + s, s, False, False)
            step(G - 2, 0, False, False)
            step(G - 1, 1, False, True)

        with nc.Block() as block:
            @block.sync
            def _(sp):
                def load(g, s):
                    sp.dma_start(x1[:, s], group(x1_g, g)).then_inc(x_loaded, 16)

                def store_xn2(g):
                    wait_alone(sp, r.xn_ready, NC // 2 * (g + 1), k.passed)
                    sp.dma_start(group(xn_g, g), xn2[:]).then_inc(xn2_stored, 16)

                def store_x2(g, s):
                    wait_alone(sp, x2_ready, NC * g + NC, k.passed)
                    sp.dma_start(group(x2_g, g), x2[:, s]).then_inc(x2_stored[s], 16)

                def step(g, s, first, last):
                    if not last:
                        wait_alone(sp, norm1_ready, g + 1, k.passed)
                        if not first:
                            wait_alone(sp, x2_ready, NC * g, k.passed)
                        load(g + 1, 1 - s)
                    if not first:
                        store_x2(g - 1, 1 - s)
                        store_xn2(g - 1)

                load(0, 0)
                rounds(sp, step)
                store_x2(G - 1, 1)
                store_xn2(G - 1)
                for s in range(2):
                    sp.wait_ge(x2_stored[s], 16 * (G // 2))
                sp.wait_ge(xn2_stored, 16 * G)

            @block.gpsimd
            def _(pool):
                def set_out(g, c):
                    wait(pool, sc_made, 4 * (NC * g + c - 1))
                    for half in range(KD):
                        pool.wait_ge(qk_low, 2 * KD * g + half + 1)
                        for part in range(2):
                            ins = pool.tensor_tensor(
                                qx[c % 2][part][:, half],
                                qkT[part][:, half, c * P:(c + 1) * P].bitcast(F32).unsqueeze(1).broadcast_to([P, HH, P]),
                                k.heads[:].unsqueeze(2).broadcast_to([P, HH, P]), ALU.mult)
                        ins.then_inc(qx_ready, 1)

                def step(g, s, first, last):
                    for c in range(1, NC):
                        set_out(g, c)
                    if not (isinstance(g, int) and g < 2):
                        r.enter(pool, g - 2, s)
                    if not last:
                        set_out(g + 1, 0)

                pool.memset(vpad[0][:], 0.0).then_inc(vzero, 1)
                pool.memset(vpad[1][:], 0.0).then_inc(vzero, 1)
                set_out(0, 0)
                rounds(pool, step)
                r.enter(pool, G - 2, 0)
                r.enter(pool, G - 1, 1)
                for s in range(2):
                    pool.wait_ge(r.entered[s], 16 * NC * TOPK * (G // 2))

            @block.tensor
            def _(pe):
                def turn(g):
                    for b in range(2):
                        pe.wait_ge(xn_ready, NC // 2 * g + b + 1)
                        for c in range(2):
                            for h in range(KD):
                                at = (h * 2 + c) * P
                                ins = pe.transpose(wide[b][:, at:at + P], xn[:, 2 * b + c, h * P:(h + 1) * P], k.ident[:])
                        ins.then_inc(turned, 1)

                def project_qk(g):
                    pe.wait_ge(xT_ready, 2 * g + 2)
                    for n in range(2 * KD):
                        if n >= 2:
                            pe.wait_ge(qk_kept, 2 * KD * g + n - 1)
                        for kk in range(KD):
                            cols = slice(n * P, (n + 1) * P)
                            ins = mm3(pe, wide[n % 2][:], (k.wqk[0][:, kk, cols], k.wqk[1][:, kk, cols]),
                                      (xT[0][:, kk, :], xT[1][:, kk, :]), kk == 0, kk == KD - 1)
                        ins.then_inc(qk_made, 1)

                def project_vk(g, c):
                    wait(pe, vk_kept, 2 * (NC * g + c))
                    rows = slice(c * P, (c + 1) * P)
                    for kk in range(KD):
                        mm3(pe, vk[:, 0:D], (xT[0][:, kk, rows], xT[1][:, kk, rows]),
                            (k.wv[0][:, kk, :], k.wv[1][:, kk, :]), kk == 0, kk == KD - 1)
                    if c == 0:
                        pe.wait_ge(qk_kept, 2 * KD * (g + 1))
                    for half in range(KD):
                        ins = pe.transpose(vk[:, D + half * P:D + (half + 1) * P], kT[:, half, rows], k.ident[:])
                    ins.then_inc(vk_made, 1)

                def scores(g, c, quarters):
                    for q in quarters:
                        half, u = q // 2, 16 * g + 4 * c + q
                        if c == 0 and q % 2 == 0:
                            pe.wait_ge(qk_low, 2 * KD * g + KD + half + 1)
                        if q % 2 == 0:
                            pe.wait_ge(qx_ready, KD * (NC * g + c) + half + 1)
                        wait(pe, prob_ready, u - 1)
                        heads = slice((q % 2) * 4, (q % 2) * 4 + 4)
                        mm3(pe, sc[q % 2][:], [t[:, KD + half, c * P:(c + 1) * P] for t in qkT],
                            [t[:, half, heads, :] for t in qx[c % 2]], True, True).then_inc(sc_made, 1)

                def vdiag(c, half):
                    at = half * HH * P
                    return vpad[c % 2][:, at:at + HH * VSTEP].rearrange("p (h x) -> p h x", x=VSTEP)[:, :, 0:HD]

                def update_state(g, c):
                    pe.wait_ge(vk_kept, 2 * (NC * g + c + 1))
                    wait(pe, state_ready, NC * g + c)
                    for half in range(KD):
                        ins = pe.matmul(kv[:, half * P:(half + 1) * P], krow[c % 2][:, half * P:(half + 1) * P],
                                        vdiag(c, half), start=True, stop=True)
                    ins.then_inc(kv_made, 1)

                def attend_state(g, c):
                    wait(pe, state_ready, NC * g + c)
                    if c == 0:
                        pe.wait_ge(fresh, g + 1)
                    wait(pe, y_ready, NC * g + c)
                    for half in range(KD):
                        pe.matmul(yt[:, half * P:(half + 1) * P], state[c % 2][:, half, :],
                                  qT[:, half, c * P:(c + 1) * P], start=(half == 0), stop=False)

                def attend_chunk(g, c):
                    for half in range(KD):
                        out = yt[:, half * P:(half + 1) * P]
                        for hh in range(HH):
                            h = half * HH + hh
                            if hh % 4 == 0:
                                pe.wait_ge(prob_ready, 16 * g + 4 * c + h // 4 + 1)
                            ins = pe.matmul(out, vpad[c % 2][:, h * P:(h + 1) * P], prob[c % 2][:, h, :],
                                            start=False, stop=(h == H - 1))
                        ins.then_inc(y_made, 1)

                def project_out(g, c):
                    pe.wait_ge(y_ready, NC * g + c + 1)
                    wait(pe, x2_ready, NC * g + c)
                    for half in range(KD):
                        ins = mm3(pe, op[:, 0:D], (yT[0][:, half, :], yT[1][:, half, :]),
                                  (k.fold[0][:, half, :], k.fold[1][:, half, :]), half == 0, half == KD - 1)
                    ins.then_inc(o_made, 1)

                def step(g, s, first, last):
                    project_vk(g, 0)
                    scores(g, 0, (0, 1))
                    if not first:
                        project_out(g - 1, 3)
                    scores(g, 0, (2, 3))
                    for c in range(NC):
                        update_state(g, c)
                        if not first and c >= 2:
                            pe.wait_ge(x2_ready, NC * g + c)
                            if c == 2:
                                r.logits(pe, g - 1)
                            else:
                                r.ranks(pe, g - 1)
                        attend_state(g, c)
                        if not last and c == 3:
                            project_qk(g + 1)
                        attend_chunk(g, c)
                        if not first and c == 1:
                            r.transposes(pe, g - 1, xn2)
                        if c < NC - 1:
                            project_vk(g, c + 1)
                            scores(g, c + 1, (0, 1))
                            if not last and c == 2:
                                turn(g + 1)
                            if not first and c == 2:
                                pe.wait_ge(r.chosen_ready, g)
                            project_out(g, c)
                            scores(g, c + 1, (2, 3))
                    if not first:
                        pe.wait_ge(r.rank_read, g)

                turn(0)
                project_qk(0)
                rounds(pe, step)
                project_out(G - 1, 3)
                r.transposes(pe, G - 1, xn2)
                pe.wait_ge(x2_ready, NC * G)
                r.logits(pe, G - 1)
                r.ranks(pe, G - 1)
                r.count(pe, G)

            @block.scalar
            def _(act):
                def keep_vk(g, c):
                    act.wait_ge(vk_made, NC * g + c + 1)
                    wait(act, y_made, KD * (NC * g + c - 1))
                    dst = vpad[c % 2]
                    for half in range(KD):
                        at = half * HH * P
                        ins = act.activation(
                            dst[:, at:at + HH * VSTEP].rearrange("p (h x) -> p h x", x=VSTEP)[:, :, 0:HD],
                            vk[:, half * P:(half + 1) * P].rearrange("p (h e) -> p h e", e=HD), ACT.Copy)
                    ins.then_inc(vk_kept, 1)
                    act.activation(krow[c % 2][:], vk[:, D:2 * D], ACT.Copy).then_inc(vk_kept, 1)

                def high_x(g):
                    for b in range(2):
                        act.wait_ge(turned, 2 * g + b + 1)
                        act.activation(xT[0][:, :, b * 2 * P:(b + 1) * 2 * P],
                                       wide[b][:].rearrange("p (h t) -> p h t", h=KD), ACT.Copy).then_inc(x_high, 1)

                def high_qk(g):
                    for n in range(2 * KD):
                        act.wait_ge(qk_made, 2 * KD * g + n + 1)
                        whole = (qT, kT)[n // KD][:, n % KD, :]
                        act.activation(whole, wide[n % 2][:], ACT.Copy).then_inc(qk_kept, 1)
                        act.wait_ge(qk_kept, 2 * KD * g + n + 1)
                        act.activation(qkT[0][:, n, :], whole, ACT.Copy).then_inc(qk_high, 1)

                def norm_x1(g, s):
                    act.wait_ge(norm1_ready, g + 1)
                    norm1.scaled(act, lambda c: x1[:, s, c, :], xn, xn_ready)

                def norm_x2(g, s):
                    act.wait_ge(norm2_ready, g + 1)
                    wait(act, xn2_stored, 16 * g)
                    norm2.scaled(act, lambda c: x2[:, s, c, :], xn2, r.xn_ready)

                def step(g, s, first, last):
                    keep_vk(g, 0)
                    for c in range(NC):
                        if not last and c == 2:
                            wait(act, r.lg_made, g)
                            norm_x1(g + 1, 1 - s)
                        if not last and c == 3:
                            high_qk(g + 1)
                        act.wait_ge(y_made, KD * (NC * g + c + 1))
                        wait(act, o_made, NC * g + c)
                        act.activation(yT[0][:], yt[:, 0:KD * P].rearrange("p (a t) -> p a t", a=KD),
                                       ACT.Copy).then_inc(y_high, 1)
                        if not first and c == 1:
                            r.keep_xnT(act, g - 1)
                        if not first and c == 2:
                            r.weigh(act, g - 1)
                        if not first and c == 0:
                            norm_x2(g - 1, 1 - s)
                        if c < NC - 1:
                            keep_vk(g, c + 1)
                        if not last and c == 2:
                            high_x(g + 1)

                norm_x1(0, 0)
                high_x(0)
                high_qk(0)
                act.wait_ge(vzero, 2)
                rounds(act, step)
                norm_x2(G - 1, 1)
                r.keep_xnT(act, G - 1)
                r.weigh(act, G - 1)

            @block.vector
            def _(dve):
                def mask(g, c, quarters):
                    wait(dve, y_made, KD * (NC * g + c - 1))
                    for q in quarters:
                        dve.wait_ge(sc_made, 16 * g + 4 * c + q + 1)
                        dve.tensor_tensor(prob[c % 2][:, 4 * q:4 * q + 4, :],
                                          sc[q % 2][:].rearrange("p (h t) -> p h t", h=4),
                                          k.causal[:].unsqueeze(1).broadcast_to([P, 4, P]), ALU.mult).then_inc(prob_ready, 1)

                def advance(g, c):
                    dve.wait_ge(kv_made, NC * g + c + 1)
                    dve.tensor_tensor(update[:], kv[:, 0:KD * P].rearrange("p (a t) -> p a t", a=KD),
                                      k.same_head[:].unsqueeze(1).broadcast_to([P, KD, P]), ALU.mult)
                    dve.drain()
                    wait(dve, y_made, KD * (NC * g + c))
                    dve.tensor_tensor(state[(c + 1) % 2][:], state[c % 2][:], update[:], ALU.add).then_inc(state_ready, 1)

                def low_y(g, c):
                    dve.wait_ge(y_high, NC * g + c + 1)
                    dve.tensor_tensor(yT[1][:], yt[:, 0:KD * P].rearrange("p (a t) -> p a t", a=KD),
                                      yT[0][:].bitcast(F32), ALU.subtract).then_inc(y_ready, 1)

                def add_out(g, s, c, i):
                    dve.wait_ge(o_made, NC * g + c + 1)
                    if c == 0:
                        wait(dve, x2_stored[s], 16 * i)
                    dve.tensor_tensor(x2[:, s, c, :], op[:, 0:D], x1[:, s, c, :], ALU.add).then_inc(x2_ready, 1)

                def low_x(g):
                    for b in range(2):
                        dve.wait_ge(x_high, 2 * g + b + 1)
                        cols = slice(b * 2 * P, (b + 1) * 2 * P)
                        dve.tensor_tensor(xT[1][:, :, cols], wide[b][:].rearrange("p (h t) -> p h t", h=KD),
                                          xT[0][:, :, cols].bitcast(F32), ALU.subtract).then_inc(xT_ready, 1)

                def low_qk(g, parts):
                    for n in parts:
                        dve.wait_ge(qk_high, 2 * KD * g + n + 1)
                        dve.tensor_tensor(qkT[1][:, n, :], (qT, kT)[n // KD][:, n % KD, :], qkT[0][:, n, :].bitcast(F32),
                                          ALU.subtract).then_inc(qk_low, 1)

                def moments_x1(g, s):
                    dve.wait_ge(x_loaded, 16 * g + 16)
                    wait(dve, xn_ready, NC // 2 * g)
                    for c in range(NC):
                        norm1.statistics(dve, x1[:, s, c, :], c)
                    norm1.moments(dve, norm1_ready)

                def stats_x2(g, s, c):
                    dve.wait_ge(x2_ready, NC * g + c + 1)
                    if c == NC - 1:
                        wait(dve, r.xn_ready, NC // 2 * g)
                    norm2.statistics(dve, x2[:, s, c, :], c)

                def step(g, s, first, last, i):
                    at = slice(g, g + 1) if isinstance(g, int) else bass.ds(g, 1)
                    wait(dve, state_ready, NC * g)
                    dve.tensor_scalar(state[0][:], state[0][:], k.later[:, at], None, ALU.mult).then_inc(fresh, 1)
                    mask(g, 0, (0, 1))
                    if not first:
                        add_out(g - 1, 1 - s, 3, i)
                    mask(g, 0, (2, 3))
                    for c in range(NC):
                        advance(g, c)
                        if not first and c == 0:
                            stats_x2(g - 1, 1 - s, 3)
                            norm2.moments(dve, norm2_ready)
                        if not last and c == 1:
                            moments_x1(g + 1, 1 - s)
                        if not first and c == 2:
                            r.choose(dve, g - 1)
                        if c == 3:
                            if not last:
                                low_qk(g + 1, (0,))
                            if not first:
                                r.place_first(dve, g - 1)
                            if not last:
                                low_qk(g + 1, (1, 2, 3))
                            if not first:
                                r.place_rest(dve, g - 1, 1 - s, 16 * NC * TOPK * (i - 1 + s))
                        low_y(g, c)
                        if c < NC - 1:
                            mask(g, c + 1, (0, 1))
                            if not last and c == 2:
                                low_x(g + 1)
                            add_out(g, s, c, i)
                            mask(g, c + 1, (2, 3))
                            stats_x2(g, s, c)

                dve.memset(state[0][:], 0.0)
                r.start(dve)
                moments_x1(0, 0)
                low_x(0)
                low_qk(0, range(2 * KD))
                step(0, 0, True, False, 0)
                step(1, 1, False, False, 0)
                with dve.Fori(1, G // 2 - 1) as i:
                    for s in range(2):
                        step(2 * i + s, s, False, False, i)
                step(G - 2, 0, False, False, G // 2 - 1)
                step(G - 1, 1, False, True, G // 2 - 1)
                add_out(G - 1, 1, 3, G // 2 - 1)
                stats_x2(G - 1, 1, 3)
                norm2.moments(dve, norm2_ready)
                r.choose(dve, G - 1)
                r.place_first(dve, G - 1)
                r.place_rest(dve, G - 1, 1, 16 * NC * TOPK * (G // 2 - 1))
                r.tiles(dve, ntile, first_tile)


class Constants:

    def __init__(self, m):
        self.ident = m.sb("ident", [P, P])
        self.before = m.sb("before", [P, P], BF16)
        self.ones = m.sb("ones", [P, P], BF16)
        self.causal = m.sb("causal", [P, P])
        self.heads = m.sb("heads", [P, HH])
        self.same_head = m.sb("same_head", [P, P])
        self.expert_i = m.sb("expert_i", [P, E], I32)
        self.region_i = m.sb("region_i", [P, E], I32)
        self.later_i = m.sb("later_i", [P, G // GB, GB], I32)
        self.token = m.sb("token", [P, T // P], I32)
        self.spare = m.sb("spare", [P, TS // P], I32)
        self.expert = m.sb("expert", [P, E])
        self.region = m.sb("region", [P, E])
        self.later = m.sb("later", [P, G])
        self.passed = m.sem("passed")
        self.wr = m.sb("wr", [P, KD, E])
        self.wqk = [m.sb(f"wqk{i}", [P, KD, 2 * D], F32R) for i in range(2)]
        self.wv = [m.sb(f"wv{i}", [P, KD, D], F32R) for i in range(2)]
        self.fold = [m.sb(f"fold{i}", [P, KD, D], F32R) for i in range(2)]


def macaron(nc, x, wqT, wkT, wvT, wcT, ltriT, wr, w1, w3, w2, out):
    xn = nc.dram_tensor("normed_rows", (ROWS, D), F32).ap()
    x1 = nc.dram_tensor("x1", (ROWS, D), F32).ap()
    tables = [nc.dram_tensor(f"table{i}", (SLOTS, 2), F32).ap() for i in range(2)]
    weights = (w1, w3, w2)
    with ExitStack() as ctx:
        m = Memory(nc, ctx, "c_")
        k = Constants(m)
        slot_a = [m.sb("wa_hi", [P, WCOLS], F32R), m.sb("wa_lo", [P, WCOLS], F32R)]
        raw_loaded = [m.sem(f"raw_loaded{b}") for b in range(2)]
        tiles = [(m.sb(f"ntile{i}", [P, E], I32), m.sb(f"first{i}", [P, E + 1], I32)) for i in range(2)]
        attention = dict(wqT=wqT, wkT=wkT, wvT=wvT, wcT=wcT, ltriT=ltriT, wr=wr)
        with ExitStack() as early:
            raw = early.enter_context(nc.sbuf_tensor("raw1", [P, WCOLS], F32))
            route_phase(nc, k, attention, x, xn, x1, out, tables, weights, slot_a, raw, raw_loaded, tiles[0])
            expert_phase(nc, k, "e1_", xn, x1, tables[0], weights, slot_a, raw, raw_loaded, tiles[0], 2)
        middle_phase(nc, k, x1, xn, out, tables[1], tiles[1])
        with ExitStack() as late:
            raw = late.enter_context(nc.sbuf_tensor("raw2", [P, WCOLS], F32))
            expert_phase(nc, k, "e2_", xn, out, tables[1], weights, slot_a, raw, raw_loaded, tiles[1], 2 + E)


def kernel(L0_attn_X, L0_attn_Wq, L0_attn_Wk, L0_attn_Wv, L0_attn_Wc, L0_attn_Ltri,
           L0_ffn_Wr, L0_ffn_W1, L0_ffn_W3, L0_ffn_W2):
    import numpy as np
    import concourse.bacc as bacc
    from concourse.bass_utils import run_bass_kernel_spmd

    shape = np.shape(L0_attn_X)
    arrays = {
        "x": np.asarray(L0_attn_X).reshape(T, D),
        "wqT": np.asarray(L0_attn_Wq).T, "wkT": np.asarray(L0_attn_Wk).T,
        "wvT": np.asarray(L0_attn_Wv).T, "wcT": np.asarray(L0_attn_Wc).T,
        "ltriT": np.asarray(L0_attn_Ltri).transpose(0, 2, 1),
        "wr": np.asarray(L0_ffn_Wr), "w1": np.asarray(L0_ffn_W1),
        "w3": np.asarray(L0_ffn_W3), "w2": np.asarray(L0_ffn_W2),
    }
    arrays = {n: np.ascontiguousarray(a) for n, a in arrays.items()}
    nc = bacc.Bacc("TRN2", target_bir_lowering=False, num_devices=1)
    args = [nc.dram_tensor(n, a.shape, mybir.dt.from_np(a.dtype), kind="ExternalInput").ap()
            for n, a in arrays.items()]
    out = nc.dram_tensor("out", (ROWS, D), F32, kind="ExternalOutput").ap()
    macaron(nc, *args, out)
    result = run_bass_kernel_spmd(nc, [arrays], core_ids=[0])
    return result.results[0]["out"][0:T].reshape(shape)
```
